# Optimizing a Trainium2 kernel written in Bass

```python
import numpy as np
import jax
import jax.numpy as jnp

def _softmax(x, axis=-1):
    return jax.nn.softmax(x, axis=axis)

def _gelu(x):
    return jax.nn.gelu(x, approximate=True)

def _silu(x):
    return jax.nn.silu(x)

def _sigmoid(x):
    return jax.nn.sigmoid(x)

def _layernorm(x, axis=-1, eps=1e-05):
    m = jnp.mean(x, axis=axis, keepdims=True)
    v = jnp.var(x, axis=axis, keepdims=True)
    return (x - m) / jnp.sqrt(v + eps)

def _scatter_add(tgt, idx, src, axis=0):
    return tgt.at[idx].add(src)

def _segment_sum(src, seg, n):
    return jax.ops.segment_sum(src, seg, n)
kernel_name = 'mk_cond_seq_d2_seqx_r4_6193a2'

def setup_inputs(seed: int=0):
    np.random.seed(seed)
    _w = jnp.asarray

    def _rec_inputs():
        import jax
        import jax.numpy as jnp
        _rk = jax.random.key(seed)
        x = -0.0002928 + 1 * jax.random.normal(jax.random.fold_in(_rk, 1), (8, 256, 256), jnp.float32)
        _lenS = 256 - jax.random.randint(jax.random.fold_in(_rk, 7), (8,), 0, max(1, 256 // 4) + 1, jnp.int32)
        _lenS2 = 256 - jax.random.randint(jax.random.fold_in(_rk, 8), (8,), 0, max(1, 256 // 4) + 1, jnp.int32)
        cond_1024 = 0.0061147 + 1.02565 * jax.random.normal(jax.random.fold_in(_rk, 11), (8, 256), jnp.float32)
        return (x, cond_1024)
    x, cond_1024 = _rec_inputs()

    def _L0_cond_setup():
        import jax, jax.numpy as jnp
        import numpy as np
        D = 256
        H = 16
        HD = 4 * D
        B, T = (4, 256)
        EPS = 1e-05

        def _layernorm(x, g, b):
            mu = jnp.mean(x, axis=-1, keepdims=True)
            var = jnp.mean(jnp.square(x - mu), axis=-1, keepdims=True)
            return (x - mu) * jax.lax.rsqrt(var + EPS) * g + b

        def _attention(x, Wqkv, Wproj, bproj):
            b, t, c = x.shape
            hd = c // H
            qkv = (x @ Wqkv).reshape(b, t, 3, H, hd).transpose(2, 0, 3, 1, 4)
            q, k, v = (qkv[0], qkv[1], qkv[2])
            scale = hd ** (-0.5)
            scores = jnp.einsum('bhqd,bhkd->bhqk', q, k) * scale
            causal = jnp.tril(jnp.ones((t, t), bool))
            scores = jnp.where(causal, scores, -jnp.inf)
            attn = jax.nn.softmax(scores, axis=-1)
            out = jnp.einsum('bhqk,bhkd->bhqd', attn, v)
            out = out.transpose(0, 2, 1, 3).reshape(b, t, c)
            return out @ Wproj + bproj
        key = jax.random.key(seed)
        ks = jax.random.split(key, 12)
        s = 0.02
        return {'x': jax.random.normal(ks[0], (B, T, D), jnp.float32), 'condition': jax.random.normal(ks[1], (B, D), jnp.float32), 'Wqkv': jax.random.normal(ks[2], (D, 3 * D), jnp.float32) * s, 'Wproj': jax.random.normal(ks[3], (D, D), jnp.float32) * s, 'bproj': jnp.zeros((D,), jnp.float32), 'W1': jax.random.normal(ks[4], (D, HD), jnp.float32) * s, 'b1': jnp.zeros((HD,), jnp.float32), 'W2': jax.random.normal(ks[5], (HD, D), jnp.float32) * s, 'b2': jnp.zeros((D,), jnp.float32), 'g1': jnp.ones((D,), jnp.float32), 'be1': jnp.zeros((D,), jnp.float32), 'g2': jnp.ones((D,), jnp.float32), 'be2': jnp.zeros((D,), jnp.float32), 'Wada': jax.random.normal(ks[6], (D, 6 * D), jnp.float32) * s, 'bada': jax.random.normal(ks[7], (6 * D,), jnp.float32) * s}
    _L0_cond_all = _L0_cond_setup()
    _L0_cond_in = {k: v for k, v in _L0_cond_all.items() if k in ('Wqkv', 'Wproj', 'bproj', 'W1', 'b1', 'W2', 'b2', 'g1', 'be1', 'g2', 'be2', 'Wada', 'bada')}
    del _L0_cond_all

    def _L1_cond_setup():
        import jax, jax.numpy as jnp
        import numpy as np
        B, L, D_MODEL, COND = (2, 512, 256, 256)
        D_STATE, EXPAND = (64, 2)
        D_INNER = EXPAND * D_MODEL
        MLP_H = 2 * D_MODEL
        EPS = 1e-05

        def _adaln(x, c, w, b):
            mod = (c @ w + b)[:, None, :]
            shift, scale, gate = jnp.split(mod, 3, axis=-1)
            mu = jnp.mean(x, axis=-1, keepdims=True)
            var = jnp.var(x, axis=-1, keepdims=True)
            normed = (x - mu) * jax.lax.rsqrt(var + EPS) * (1.0 + scale) + shift
            return (normed, gate)

        def _ssm(h, in_w, xproj_w, dt_bias, A_log, Dskip, out_w):
            xz = h @ in_w
            xs, z = jnp.split(xz, 2, axis=-1)
            xs = jax.nn.silu(xs)
            proj = xs @ xproj_w
            dt = jax.nn.softplus(proj[..., :D_INNER] + dt_bias)
            Bm = proj[..., D_INNER:D_INNER + D_STATE]
            Cm = proj[..., D_INNER + D_STATE:]
            A = -jnp.exp(A_log)

            def step(hst, ins):
                dt_t, B_t, C_t, x_t = ins
                dA = jnp.exp(dt_t[:, :, None] * A)
                hst = hst * dA + (dt_t * x_t)[:, :, None] * B_t[:, None, :]
                y_t = jnp.einsum('bds,bs->bd', hst, C_t)
                return (hst, y_t)
            tm = lambda a: jnp.swapaxes(a, 0, 1)
            h0 = jnp.zeros((h.shape[0], D_INNER, D_STATE), h.dtype)
            _, ys = jax.lax.scan(step, h0, (tm(dt), tm(Bm), tm(Cm), tm(xs)))
            y = jnp.swapaxes(ys, 0, 1) + xs * Dskip
            return y * jax.nn.silu(z) @ out_w
        key = jax.random.key(seed)
        ks = jax.random.split(key, 24)
        p = lambda i, shape, s=0.02: jax.random.normal(ks[i], shape, jnp.float32) * s
        inp = {'x': jax.random.normal(ks[0], (B, L, D_MODEL), jnp.float32), 'c': jax.random.normal(ks[1], (B, COND), jnp.float32), 'adaln_mamba_w': p(2, (COND, 3 * D_MODEL)), 'adaln_mamba_b': jnp.zeros((3 * D_MODEL,), jnp.float32), 'adaln_mlp_w': p(3, (COND, 3 * D_MODEL)), 'adaln_mlp_b': jnp.zeros((3 * D_MODEL,), jnp.float32), 'mlp_w1': p(4, (D_MODEL, MLP_H)), 'mlp_w2': p(5, (D_MODEL, MLP_H)), 'mlp_w3': p(6, (MLP_H, D_MODEL))}
        a_init = jnp.log(jnp.tile(jnp.arange(1, D_STATE + 1, dtype=jnp.float32), (D_INNER, 1)))
        for j, pre in enumerate(['fwd', 'bwd']):
            o = 7 + 6 * j
            inp[f'{pre}_in_w'] = p(o, (D_MODEL, 2 * D_INNER))
            inp[f'{pre}_xproj_w'] = p(o + 1, (D_INNER, D_INNER + 2 * D_STATE))
            inp[f'{pre}_dt_bias'] = jnp.zeros((D_INNER,), jnp.float32)
            inp[f'{pre}_A_log'] = a_init
            inp[f'{pre}_D'] = jnp.ones((D_INNER,), jnp.float32)
            inp[f'{pre}_out_w'] = p(o + 2, (D_INNER, D_MODEL))
        return inp
    _L1_cond_all = _L1_cond_setup()
    _L1_cond_in = {k: v for k, v in _L1_cond_all.items() if k in ('adaln_mamba_w', 'adaln_mamba_b', 'adaln_mlp_w', 'adaln_mlp_b', 'mlp_w1', 'mlp_w2', 'mlp_w3', 'fwd_in_w', 'fwd_xproj_w', 'fwd_dt_bias', 'fwd_A_log', 'fwd_D', 'fwd_out_w', 'bwd_in_w', 'bwd_xproj_w', 'bwd_dt_bias', 'bwd_A_log', 'bwd_D', 'bwd_out_w')}
    del _L1_cond_all
    return {'x': x, 'cond_1024': cond_1024, 'L0_cond_Wqkv': _L0_cond_in['Wqkv'], 'L0_cond_Wproj': _L0_cond_in['Wproj'], 'L0_cond_bproj': _L0_cond_in['bproj'], 'L0_cond_W1': _L0_cond_in['W1'], 'L0_cond_b1': _L0_cond_in['b1'], 'L0_cond_W2': _L0_cond_in['W2'], 'L0_cond_b2': _L0_cond_in['b2'], 'L0_cond_g1': _L0_cond_in['g1'], 'L0_cond_be1': _L0_cond_in['be1'], 'L0_cond_g2': _L0_cond_in['g2'], 'L0_cond_be2': _L0_cond_in['be2'], 'L0_cond_Wada': _L0_cond_in['Wada'], 'L0_cond_bada': _L0_cond_in['bada'], 'L1_cond_adaln_mamba_w': _L1_cond_in['adaln_mamba_w'], 'L1_cond_adaln_mamba_b': _L1_cond_in['adaln_mamba_b'], 'L1_cond_adaln_mlp_w': _L1_cond_in['adaln_mlp_w'], 'L1_cond_adaln_mlp_b': _L1_cond_in['adaln_mlp_b'], 'L1_cond_mlp_w1': _L1_cond_in['mlp_w1'], 'L1_cond_mlp_w2': _L1_cond_in['mlp_w2'], 'L1_cond_mlp_w3': _L1_cond_in['mlp_w3'], 'L1_cond_fwd_in_w': _L1_cond_in['fwd_in_w'], 'L1_cond_fwd_xproj_w': _L1_cond_in['fwd_xproj_w'], 'L1_cond_fwd_dt_bias': _L1_cond_in['fwd_dt_bias'], 'L1_cond_fwd_A_log': _L1_cond_in['fwd_A_log'], 'L1_cond_fwd_D': _L1_cond_in['fwd_D'], 'L1_cond_fwd_out_w': _L1_cond_in['fwd_out_w'], 'L1_cond_bwd_in_w': _L1_cond_in['bwd_in_w'], 'L1_cond_bwd_xproj_w': _L1_cond_in['bwd_xproj_w'], 'L1_cond_bwd_dt_bias': _L1_cond_in['bwd_dt_bias'], 'L1_cond_bwd_A_log': _L1_cond_in['bwd_A_log'], 'L1_cond_bwd_D': _L1_cond_in['bwd_D'], 'L1_cond_bwd_out_w': _L1_cond_in['bwd_out_w']}

def reference(x, cond_1024, L0_cond_Wqkv, L0_cond_Wproj, L0_cond_bproj, L0_cond_W1, L0_cond_b1, L0_cond_W2, L0_cond_b2, L0_cond_g1, L0_cond_be1, L0_cond_g2, L0_cond_be2, L0_cond_Wada, L0_cond_bada, L1_cond_adaln_mamba_w, L1_cond_adaln_mamba_b, L1_cond_adaln_mlp_w, L1_cond_adaln_mlp_b, L1_cond_mlp_w1, L1_cond_mlp_w2, L1_cond_mlp_w3, L1_cond_fwd_in_w, L1_cond_fwd_xproj_w, L1_cond_fwd_dt_bias, L1_cond_fwd_A_log, L1_cond_fwd_D, L1_cond_fwd_out_w, L1_cond_bwd_in_w, L1_cond_bwd_xproj_w, L1_cond_bwd_dt_bias, L1_cond_bwd_A_log, L1_cond_bwd_D, L1_cond_bwd_out_w):
    import jax
    import jax.numpy as jnp

    def _L0_cond_ref(x, condition, Wqkv, Wproj, bproj, W1, b1, W2, b2, g1, be1, g2, be2, Wada, bada):
        import jax, jax.numpy as jnp
        import numpy as np
        D = 256
        H = 16
        HD = 4 * D
        B, T = (4, 256)
        EPS = 1e-05

        def _layernorm(x, g, b):
            mu = jnp.mean(x, axis=-1, keepdims=True)
            var = jnp.mean(jnp.square(x - mu), axis=-1, keepdims=True)
            return (x - mu) * jax.lax.rsqrt(var + EPS) * g + b

        def _attention(x, Wqkv, Wproj, bproj):
            b, t, c = x.shape
            hd = c // H
            qkv = (x @ Wqkv).reshape(b, t, 3, H, hd).transpose(2, 0, 3, 1, 4)
            q, k, v = (qkv[0], qkv[1], qkv[2])
            scale = hd ** (-0.5)
            scores = jnp.einsum('bhqd,bhkd->bhqk', q, k) * scale
            causal = jnp.tril(jnp.ones((t, t), bool))
            scores = jnp.where(causal, scores, -jnp.inf)
            attn = jax.nn.softmax(scores, axis=-1)
            out = jnp.einsum('bhqk,bhkd->bhqd', attn, v)
            out = out.transpose(0, 2, 1, 3).reshape(b, t, c)
            return out @ Wproj + bproj
        mod = jax.nn.silu(condition) @ Wada + bada
        sh_a, sc_a, gt_a, sh_m, sc_m, gt_m = jnp.split(mod, 6, axis=1)
        xn = _layernorm(x, g1, be1)
        xm = xn * (1.0 + sc_a[:, None, :]) + sh_a[:, None, :]
        x = x + gt_a[:, None, :] * _attention(xm, Wqkv, Wproj, bproj)
        xn = _layernorm(x, g2, be2)
        xm = xn * (1.0 + sc_m[:, None, :]) + sh_m[:, None, :]
        h = jax.nn.gelu(xm @ W1 + b1, approximate=False)
        x = x + gt_m[:, None, :] * (h @ W2 + b2)
        return x

    def _L1_cond_ref(x, c, adaln_mamba_w, adaln_mamba_b, adaln_mlp_w, adaln_mlp_b, mlp_w1, mlp_w2, mlp_w3, fwd_in_w, fwd_xproj_w, fwd_dt_bias, fwd_A_log, fwd_D, fwd_out_w, bwd_in_w, bwd_xproj_w, bwd_dt_bias, bwd_A_log, bwd_D, bwd_out_w):
        import jax, jax.numpy as jnp
        import numpy as np
        B, L, D_MODEL, COND = (2, 512, 256, 256)
        D_STATE, EXPAND = (64, 2)
        D_INNER = EXPAND * D_MODEL
        MLP_H = 2 * D_MODEL
        EPS = 1e-05

        def _adaln(x, c, w, b):
            mod = (c @ w + b)[:, None, :]
            shift, scale, gate = jnp.split(mod, 3, axis=-1)
            mu = jnp.mean(x, axis=-1, keepdims=True)
            var = jnp.var(x, axis=-1, keepdims=True)
            normed = (x - mu) * jax.lax.rsqrt(var + EPS) * (1.0 + scale) + shift
            return (normed, gate)

        def _ssm(h, in_w, xproj_w, dt_bias, A_log, Dskip, out_w):
            xz = h @ in_w
            xs, z = jnp.split(xz, 2, axis=-1)
            xs = jax.nn.silu(xs)
            proj = xs @ xproj_w
            dt = jax.nn.softplus(proj[..., :D_INNER] + dt_bias)
            Bm = proj[..., D_INNER:D_INNER + D_STATE]
            Cm = proj[..., D_INNER + D_STATE:]
            A = -jnp.exp(A_log)

            def step(hst, ins):
                dt_t, B_t, C_t, x_t = ins
                dA = jnp.exp(dt_t[:, :, None] * A)
                hst = hst * dA + (dt_t * x_t)[:, :, None] * B_t[:, None, :]
                y_t = jnp.einsum('bds,bs->bd', hst, C_t)
                return (hst, y_t)
            tm = lambda a: jnp.swapaxes(a, 0, 1)
            h0 = jnp.zeros((h.shape[0], D_INNER, D_STATE), h.dtype)
            _, ys = jax.lax.scan(step, h0, (tm(dt), tm(Bm), tm(Cm), tm(xs)))
            y = jnp.swapaxes(ys, 0, 1) + xs * Dskip
            return y * jax.nn.silu(z) @ out_w
        h, gate = _adaln(x, c, adaln_mamba_w, adaln_mamba_b)
        h_fwd = _ssm(h, fwd_in_w, fwd_xproj_w, fwd_dt_bias, fwd_A_log, fwd_D, fwd_out_w)
        h_bwd = jnp.flip(_ssm(jnp.flip(h, 1), bwd_in_w, bwd_xproj_w, bwd_dt_bias, bwd_A_log, bwd_D, bwd_out_w), 1)
        x = x + gate * (h_fwd + h_bwd)
        h, gate = _adaln(x, c, adaln_mlp_w, adaln_mlp_b)
        mlp_out = jax.nn.silu(h @ mlp_w1) * (h @ mlp_w2) @ mlp_w3
        return x + gate * mlp_out
    x = _L0_cond_ref(x, cond_1024, L0_cond_Wqkv, L0_cond_Wproj, L0_cond_bproj, L0_cond_W1, L0_cond_b1, L0_cond_W2, L0_cond_b2, L0_cond_g1, L0_cond_be1, L0_cond_g2, L0_cond_be2, L0_cond_Wada, L0_cond_bada)
    x = _L1_cond_ref(x, cond_1024, L1_cond_adaln_mamba_w, L1_cond_adaln_mamba_b, L1_cond_adaln_mlp_w, L1_cond_adaln_mlp_b, L1_cond_mlp_w1, L1_cond_mlp_w2, L1_cond_mlp_w3, L1_cond_fwd_in_w, L1_cond_fwd_xproj_w, L1_cond_fwd_dt_bias, L1_cond_fwd_A_log, L1_cond_fwd_D, L1_cond_fwd_out_w, L1_cond_bwd_in_w, L1_cond_bwd_xproj_w, L1_cond_bwd_dt_bias, L1_cond_bwd_A_log, L1_cond_bwd_D, L1_cond_bwd_out_w)
    return x

_drawn_inputs = setup_inputs


def setup_inputs(seed=0):
    import zlib

    import numpy as np

    out = dict(_drawn_inputs(seed))
    spreads = {'L0_cond_bproj': (0.0, 0.1),
     'L0_cond_b1': (0.0, 0.1),
     'L0_cond_b2': (0.0, 0.1),
     'L0_cond_g1': (1.0, 0.2),
     'L0_cond_be1': (0.0, 0.1),
     'L0_cond_g2': (1.0, 0.2),
     'L0_cond_be2': (0.0, 0.1),
     'L1_cond_adaln_mamba_b': (0.0, 0.1),
     'L1_cond_adaln_mlp_b': (0.0, 0.1),
     'L1_cond_fwd_dt_bias': (0.0, 0.1),
     'L1_cond_fwd_D': (1.0, 0.2),
     'L1_cond_bwd_dt_bias': (0.0, 0.1),
     'L1_cond_bwd_D': (1.0, 0.2)}
    factors = {}
    for name, (base, spread) in spreads.items():
        noise = np.random.default_rng([zlib.crc32(name.encode()), seed]).standard_normal(out[name].shape)
        drawn = base * np.exp(spread * noise) if base else spread * noise
        out[name] = jnp.asarray(drawn.astype(out[name].dtype))
    for name, factor in factors.items():
        out[name] = (out[name] * factor).astype(out[name].dtype)
    return out
```

```python
import numpy as np
import concourse.bass as bass
from concourse import mybir
from contextlib import ExitStack


class Flow:

    def __init__(self, sem, per, start=0):
        self.sem, self.per, self.start = sem, per, start

    def at(self, rnd, k):
        return rnd * self.per + (self.start + k)


def cond_transformer_mamba_kernel(
    nc, x, columns, rows, A_log, Wqkv, Wproj, W1, W2, Wada, wmamba, wglu, glu_w1, glu_w2, glu_w3,
    f_in, f_xproj, f_out, b_in, b_xproj, b_out, out, gate_rows,
):
    f32, bf16 = mybir.dt.float32, mybir.dt.bfloat16
    ALU, ACT, AX = mybir.AluOpType, mybir.ActivationFunctionType, mybir.AxisListType

    P = 128
    B, T, D = x.shape
    H = 16
    HD = D // H
    HP = 32
    KD = D // P
    NB = 512
    BB = NB // T
    NBLK = B * T // NB
    TT = NB // P
    QT = T // P
    KF = W1.shape[1] // P
    DI = f_out.shape[0]
    KI = DI // P
    NS = A_log.shape[1] // (2 * KI)
    KG = glu_w1.shape[1] // P
    EPS = 1e-5
    NR = 4
    NEG = -1e30
    LN_ATT, LN_MLP, LN_SSM, LN_GLU = range(4)
    RES_ATT, RES_MLP, RES_SSM, RES_GLU = 0, 1, 2, 4
    GATE_OF = {0: 0, 1: 1, 2: 2, 3: 2, 4: 3}
    GH = 2
    GT = H // GH
    NG = BB * QT * GT

    x_tiles = x.rearrange("b (h p) d -> p (b h) d", p=P)
    out_tiles = out.rearrange("b (h p) d -> p (b h) d", p=P)

    ctx = ExitStack()
    with ctx:
        def sb(name, shape, dt=f32):
            return ctx.enter_context(nc.sbuf_tensor(name, shape, dt))

        def flow(name, per, start=0):
            return Flow(ctx.enter_context(nc.semaphore(name)), per, start)

        wq = sb("wq", [P, KD, H, HP])
        wk = sb("wk", [P, KD, H, HP])
        wv = sb("wv", [P, KD, D])
        wproj = sb("wproj", [P, KD, D])
        w1 = sb("w1", [P, KD, KF * P])
        w2 = sb("w2", [P, KF, D])
        w_in = [sb(f"w_in{d}", [P, KD, 2 * DI]) for d in range(2)]
        w_xp = [sb(f"w_xp{d}", [P, KI, DI + 2 * NS]) for d in range(2)]
        w_out = [sb(f"w_out{d}", [P, KI, D]) for d in range(2)]
        wg1 = sb("wg1", [P, KD, KG * P])
        wg2 = sb("wg2", [P, KD, KG * P])
        wg3 = sb("wg3", [P, KG, D])
        row_in = sb("row_in", [1, rows.shape[1]])
        gate_bias = row_in[:, 0:4 * D].rearrange("a (i n) -> a i n", n=D)
        bias_rows = row_in[:, 4 * D:6 * D].rearrange("a (i n) -> a i n", n=D)
        col_in = sb("col_in", [P, columns.shape[1]])
        cols = [0]

        def column(*shape):
            at, n = cols[0], int(np.prod(shape))
            cols[0] += n
            part = col_in[:, at:at + n]
            return part if len(shape) == 1 else part.rearrange("p (a b) -> p a b", b=shape[1])

        cond_col = column(KD, B)
        mod_bias = column(8, KD)
        ln_g, ln_b = column(2, KD), column(2, KD)
        b1_col = column(KF)
        dtb_col, D_col = column(2, KI), column(2, KI)
        A = sb("A", [P, 2, KI, NS])
        ident = sb("ident", [P, P])
        ident_b = sb("ident_b", [P, P], bf16)
        causal_b = sb("causal_b", [P, P], bf16)
        ones_row = sb("ones_row", [1, P])
        skip_diag = sb("skip_diag", [P, 2, KI, P])
        silu_col = sb("silu_col", [P, KD, B])
        mods = sb("mods", [P, 8, KD, B])
        mod_scale = sb("mod_scale", [P, 4, KD, B])
        mod_shift = sb("mod_shift", [P, 4, KD, B])
        gate = sb("gate", [P, BB, 4, D])
        xs_all = sb("xs_all", [P, B * QT, D])
        xn = sb("xn", [P, TT, D])
        hT = sb("hT", [P, KD, NB])
        stats = sb("stats", [P, TT, 6])
        mv = sb("mv", [P, TT, 2])
        rstd = sb("rstd", [P, TT])
        qT = sb("qT", [P, KI, NB])
        kT = sb("kT", [P, KI, NB])
        v = sb("v", [P, TT, D])
        probs = sb("probs", [P, 4, GH, T])
        probsT = sb("probsT", [P, 4, QT, GH, P])
        prime = sb("prime", [P, 5])
        nmax = sb("nmax", [P, 4, GH])
        psum_exp = sb("psum_exp", [P, TT, H])
        rsum = sb("rsum", [P, TT, H])
        inner = sb("inner", [P, 2 * KI, NB])
        dto = sb("dto", [P, KI, NB])
        B_sb = sb("B_sb", [P, NR, NB])
        bc_parts = sb("bc_parts", [P, 3, NB], bf16)
        bc_rest = sb("bc_rest", [P, NB])

        o_sb = dto[:, 0:2, :].rearrange("p a (b d) -> p (a b) d", d=D)
        oT = dto[:, 2:4, :]
        xsT, szT = inner[:, 0:KI, :], inner[:, KI:2 * KI, :]
        dt = dto
        u = probsT[:, :, :, :, :].rearrange("p a b c d -> p a (b c d)")
        uB = probs[:, :, :, :].rearrange("p (r a) b t -> p r a (b t)", r=2)
        as_pair = lambda t: t[:, :, :].rearrange("p a b -> p (a b)").rearrange("p (e n) -> p e n", n=NB)
        hst = [kT[:, 0:2, :], kT[:, 2:4, :], as_pair(xn), as_pair(v)]
        hC = qT[:, :, :].rearrange("p (a e) n -> p a e n", a=2)
        wada = inner[:, 0:6, :].rearrange("p a b -> p (a b)").rearrange("p (k n) -> p k n", k=KD)
        wada1 = [t[:, 0:3, :].rearrange("p a b -> p (a b)").rearrange("p (k n) -> p k n", k=KD) for t in (qT, kT)]
        mod_rows = dto[0:B, 0:2, :].rearrange("p a b -> p (a b)")

        ps = ctx.enter_context(nc.psum_tensor("ps", [P, 8, NB], f32))
        BANK_C, BANK_B, BANK_Y = 2, 3, 4

        mods_in, x_in, weights_in = (ctx.enter_context(nc.semaphore(n)) for n in ("mods_in", "x_in", "weights_in"))
        pool_step, dve_setup, silu_ready, mods_mm, rows_ready, rows_out, consts_ready, mods_ready, A_ready = (
            ctx.enter_context(nc.semaphore(n)) for n in
            ("pool_step", "dve_setup", "silu_ready", "mods_mm", "rows_ready", "rows_out", "consts_ready",
             "mods_ready", "A_ready"))
        bn_turns = ctx.enter_context(nc.semaphore("bn_turns"))
        pads_zero = ctx.enter_context(nc.semaphore("pads_zero"))
        gate_in = flow("gate_in", 16)
        out_done = ctx.enter_context(nc.semaphore("out_done"))
        DVE_STEPS = 38
        dve_step = flow("dve_step", DVE_STEPS)
        stat_ready, std_ready, xn_ready = flow("stat_ready", 4), flow("std_ready", 4), flow("xn_ready", 4)
        xnT_mm, hT_ready = flow("xnT_mm", 8), flow("hT_ready", 8)
        q_mm, k_mm, v_mm = flow("q_mm", 4), flow("k_mm", 4), flow("v_mm", 2)
        q_ready, k_ready, v_ready = flow("q_ready", 4), flow("k_ready", 4), flow("v_ready", 2)
        score_mm, max_ready, probs_ready = flow("score_mm", NG), flow("max_ready", NG), flow("probs_ready", GH * NG)
        probsT_mm, probsT_ready, pv_mm = flow("probsT_mm", NG), flow("probsT_ready", NG), flow("pv_mm", NG)
        o_ready, oT_mm, oT_ready = flow("o_ready", TT), flow("oT_mm", 2), flow("oT_ready", 2)
        res_mm, res_done = flow("res_mm", 5 * BB), flow("res_done", 5 * BB)
        up_mm, gelu_ready = flow("up_mm", KF), flow("gelu_ready", KF)
        in_mm, in_ready = flow("in_mm", 4 * KI), flow("in_ready", 4 * KI)
        xp_mm, pre_ready, bc_ready = flow("xp_mm", 2 * (KI + 1)), flow("pre_ready", 2 * KI), flow("bc_ready", 2)
        abs_ready, exp_ready, one_ready, log_ready = (flow(n, 2) for n in
                                                      ("abs_ready", "exp_ready", "one_ready", "log_ready"))
        dt_ready, u_ready, reset_ready, g_ready = (flow(n, 2) for n in ("dt_ready", "u_ready", "reset_ready", "g_ready"))
        glu_mm, glu_silu, glu_ready = flow("glu_mm", 2 * KG), flow("glu_silu", KG), flow("glu_ready", KG)
        B_mm, C_mm, B_ready = flow("B_mm", 1), flow("C_mm", 1), flow("B_ready", 1, 1)
        dA_ready, uB_ready = flow("dA_ready", 4), flow("uB_ready", 2, 2 * NR)
        scan_done, hC_ready, y_mm = flow("scan_done", 4, 4), flow("hC_ready", 2, 2), flow("y_mm", 2, 2)

        block = ctx.enter_context(nc.Block())

        @block.sync
        def _(sp):
            sp.dma_start(col_in[:, :], columns).then_inc(mods_in, 16)
            sp.dma_start(row_in[:, :], rows).then_inc(mods_in, 16)
            sp.dma_start(wada, Wada.rearrange("(k p) n -> p k n", p=P)).then_inc(mods_in, 16)
            sp.dma_start(wada1[0], wmamba.rearrange("(k p) n -> p k n", p=P)).then_inc(mods_in, 16)
            sp.dma_start(wada1[1], wglu.rearrange("(k p) n -> p k n", p=P)).then_inc(mods_in, 16)
            sp.dma_start(xs_all[:, :, :], x_tiles).then_inc(x_in, 16)
            sp.wait_ge(pads_zero, 2)
            for w, c in ((wq, 0), (wk, 1)):
                for k in range(KD):
                    sp.dma_start(w[:, k, :, 0:HD], Wqkv[k * P:(k + 1) * P, c * D:(c + 1) * D]
                                 .rearrange("p (h e) -> p h e", e=HD)).then_inc(weights_in, 16)
            sp.dma_start(wv[:, :, :], Wqkv[:, 2 * D:3 * D].rearrange("(k p) n -> p k n", p=P)).then_inc(weights_in, 16)
            loads = [(wproj, Wproj), (w1, W1), (w2, W2), (w_in[0], f_in), (w_in[1], b_in), (w_xp[0], f_xproj),
                     (w_xp[1], b_xproj), (w_out[0], f_out), (w_out[1], b_out), (wg1, glu_w1), (wg2, glu_w2), (wg3, glu_w3)]
            for w, src in loads:
                sp.dma_start(w[:, :, :], src.rearrange("(k p) n -> p k n", p=P)).then_inc(weights_in, 16)
            sp.dma_start(A[:, :, :, :].rearrange("p d k n -> p (d k n)"), A_log).then_inc(weights_in, 16)
            sp.wait_ge(rows_ready, 1)
            sp.dma_start(gate_rows, mod_rows).then_inc(rows_out, 16)
            sp.wait_ge(rows_out, 16)
            sp.dma_start(gate[:, :, :, :].rearrange("p b g d -> p b (g d)"),
                         gate_rows[0:BB, :].partition_broadcast(P)).then_inc(gate_in.sem, 16)
            with sp.Fori(0, NBLK - 1) as blk:
                sp.wait_ge(res_done.sem, res_done.at(blk, 5 * BB))
                sp.dma_start(out_tiles[:, bass.ds(blk * TT, TT), :], xs_all[:, bass.ds(blk * TT, TT), :]).then_inc(out_done, 16)
                sp.dma_start(gate[:, :, :, :].rearrange("p b g d -> p b (g d)"),
                             gate_rows[bass.ds((blk + 1) * BB, BB), :].partition_broadcast(P)).then_inc(gate_in.sem, 16)
            sp.wait_ge(res_done.sem, res_done.at(NBLK - 1, 5 * BB))
            sp.dma_start(out_tiles[:, (NBLK - 1) * TT:, :], xs_all[:, (NBLK - 1) * TT:, :]).then_inc(out_done, 16)
            sp.wait_ge(out_done, 16 * NBLK)

        N_MODS, N_WEIGHTS = 16 * 5, 16 * (5 + 12 + 1)

        @block.gpsimd
        def _(pool):
            pool.memset(wq[:, :, :, :], 0.0).then_inc(pads_zero, 1)
            pool.memset(wk[:, :, :, :], 0.0).then_inc(pads_zero, 1)
            pool.memset(ident[:, :], 0.0).then_inc(pool_step, 1)
            pool.memset(causal_b[:, :], 0.0).then_inc(pool_step, 1)
            pool.wait_ge(pool_step, 2)
            pool.affine_select(out=ident[:, :], in_=ident[:, :], compare_op=ALU.not_equal, fill=1.0, base=0,
                               pattern=[[-1, P]], channel_multiplier=1).then_inc(consts_ready, 1)
            pool.affine_select(out=causal_b[:, :], in_=causal_b[:, :], compare_op=ALU.is_ge, fill=NEG, base=0,
                               pattern=[[-1, P]], channel_multiplier=1).then_inc(consts_ready, 1)
            pool.memset(ones_row[:, :], 1.0).then_inc(consts_ready, 1)
            pool.wait_ge(consts_ready, 3)
            pool.tensor_copy(ident_b[:, :], ident[:, :]).then_inc(consts_ready, 1)
            with pool.Fori(0, NBLK) as blk:
                for d in range(2):
                    with pool.Fori(0, NS, NR) as n0:
                        for i in range(NR):
                            r = (blk * 2 + d) * NS + n0 + i
                            pool.wait_ge(B_ready.sem, B_ready.at(r, 1))
                            for pr in range(2):
                                pool.wait_ge(scan_done.sem, scan_done.at(r, 2 * pr - 2))
                                pool.tensor_tensor(uB[:, pr], u[:, 2 * pr:2 * pr + 2, :],
                                                   B_sb[:, i:i + 1, :].to_broadcast([P, 2, NB]), ALU.mult
                                                   ).then_inc(uB_ready.sem, 1)

        @block.scalar
        def _(act):
            act.wait_ge(mods_in, N_MODS)
            act.activation(silu_col[:, :, :], cond_col, ACT.Silu).then_inc(silu_ready, 1)
            act.wait_ge(weights_in, N_WEIGHTS)
            act.activation(A[:, :, :, :], A[:, :, :, :], ACT.Exp).then_inc(A_ready, 1)
            act.activation(prime[:, 4:5], col_in[:, 0:1], ACT.Copy).then_inc(B_ready.sem, 1)
            act.wait_ge(A_ready, 2)
            act.wait_ge(mods_ready, 1)

            def layernorm(blk, s):
                act.wait_ge(stat_ready.sem, stat_ready.at(blk, s + 1))
                act.activation(rstd[:, :], mv[:, :, 1], ACT.Sqrt).then_inc(std_ready.sem, 1)
                for c in range(KD):
                    act.wait_ge(xnT_mm.sem, xnT_mm.at(blk, KD * s + c + 1))
                    for b in range(BB):
                        col = bass.ds(blk * BB + b, 1)
                        last = act.activation(hT[:, c, b * T:(b + 1) * T], ps[:, c, b * T:(b + 1) * T], ACT.Identity,
                                              bias=mod_shift[:, s, c, col], scale=mod_scale[:, s, c, col])
                    last.then_inc(hT_ready.sem, 1)

            with act.Fori(0, NBLK) as blk:
                layernorm(blk, LN_ATT)
                for m in range(KI):
                    act.wait_ge(q_mm.sem, q_mm.at(blk, m + 1))
                    act.activation(qT[:, m, :], ps[:, 2 + m, :], ACT.Copy, scale=float(HD) ** -0.5).then_inc(q_ready.sem, 1)
                for g in range(NG):
                    ti, hg, s = g // GT, g % GT, g % 4
                    keys = P * (ti % QT + 1)
                    act.wait_ge(max_ready.sem, max_ready.at(blk, g + 1))
                    if g >= 4:
                        act.wait_ge(probsT_mm.sem, probsT_mm.at(blk, g - 3))
                    for i in range(GH):
                        h = GH * hg + i
                        act.activation(probs[:, s, i, 0:keys], ps[:, GH * (g % 2) + i, 0:keys], ACT.Exp, bias=nmax[:, s, i:i + 1],
                                       accum_out=psum_exp[:, ti, h:h + 1]).then_inc(probs_ready.sem, 1)
                for c in range(KD):
                    act.wait_ge(oT_mm.sem, oT_mm.at(blk, c + 1))
                    act.activation(oT[:, c, :], ps[:, c, :], ACT.Copy).then_inc(oT_ready.sem, 1)
                layernorm(blk, LN_MLP)
                for m in range(KF):
                    act.wait_ge(up_mm.sem, up_mm.at(blk, m + 1))
                    act.activation(inner[:, m, :], ps[:, (2 + m) % 8, :], ACT.Gelu, bias=b1_col[:, m:m + 1]).then_inc(gelu_ready.sem, 1)
                layernorm(blk, LN_SSM)
                for d in range(2):
                    for m in range(2 * KI):
                        act.wait_ge(in_mm.sem, in_mm.at(blk, 2 * KI * d + m + 1))
                        act.activation(inner[:, m, :], ps[:, (2 + m) % 8, :], ACT.Silu).then_inc(in_ready.sem, 1)
                    for m in range(KI):
                        act.wait_ge(xp_mm.sem, xp_mm.at(blk, (KI + 1) * d + m + 2))
                        act.activation(qT[:, m, :], ps[:, 3 + m, :], ACT.Identity, bias=dtb_col[:, d, m:m + 1]).then_inc(pre_ready.sem, 1)
                    act.wait_ge(abs_ready.sem, abs_ready.at(blk, d + 1))
                    act.activation(kT[:, :, :], kT[:, :, :], ACT.Exp).then_inc(exp_ready.sem, 1)
                    act.wait_ge(one_ready.sem, one_ready.at(blk, d + 1))
                    act.activation(dt[:, :, :], u, ACT.Ln).then_inc(log_ready.sem, 1)
                    act.wait_ge(u_ready.sem, u_ready.at(blk, d + 1))
                    act.wait_ge(reset_ready.sem, reset_ready.at(blk, d + 1))
                    lo, hi = (1, T) if d == 0 else (0, T - 1)

                    def take_B(r, slot):
                        act.wait_ge(B_mm.sem, B_mm.at(r, 1))
                        act.wait_ge(uB_ready.sem, uB_ready.at(r, 2 - 2 * NR))
                        act.activation(B_sb[:, slot, :], ps[:, BANK_B, :], ACT.Copy).then_inc(B_ready.sem, 1)

                    def decays(r, n, c):
                        act.wait_ge(scan_done.sem, scan_done.at(r, c - 1))
                        act.activation(ps[:, c % 2, :].rearrange("p (b t) -> p b t", b=BB)[:, :, lo:hi],
                                       dt[:, c, :].rearrange("p (b t) -> p b t", b=BB)[:, :, lo:hi], ACT.Exp,
                                       scale=A[:, d, c, bass.ds(n, 1)]).then_inc(dA_ready.sem, 1)

                    def state(n, slot, more=True):
                        r = (blk * 2 + d) * NS + n
                        decays(r, n, 0)
                        decays(r, n, 1)
                        if more:
                            take_B(r + 3, slot)
                        decays(r, n, 2)
                        decays(r, n, 3)

                    for i in range(NR - 1):
                        take_B((blk * 2 + d) * NS + i, i)
                    with act.Fori(0, NS - NR, NR) as n0:
                        for i in range(NR):
                            state(n0 + i, (i + 3) % NR)
                    for i in range(NR):
                        state(NS - NR + i, (i + 3) % NR, i < NR - 3)
                layernorm(blk, LN_GLU)
                for m in range(KG):
                    act.wait_ge(glu_mm.sem, glu_mm.at(blk, m + 1))
                    act.activation(inner[:, m, :], ps[:, 2 + m, :], ACT.Silu).then_inc(glu_silu.sem, 1)

        @block.vector
        def _(dve):
            setup = [0]

            def first(ins):
                setup[0] += 1
                ins.then_inc(dve_setup, 1)
                dve.wait_ge(dve_setup, setup[0])

            dve.memset(prime[:, 0:1], 0.0).then_inc(scan_done.sem, 4)
            dve.memset(prime[:, 1:2], 0.0).then_inc(hC_ready.sem, 2)
            dve.memset(prime[:, 2:3], 0.0).then_inc(y_mm.sem, 2)
            dve.memset(prime[:, 3:4], 0.0).then_inc(uB_ready.sem, 2 * NR)
            dve.wait_ge(mods_mm, 1)
            dve.wait_ge(mods_in, N_MODS)
            dve.tensor_copy(mod_rows, ps[0:B, 1:3, :].rearrange("p a n -> p (a n)")).then_inc(rows_ready, 1)
            first(dve.tensor_tensor(mods[:, :, :, :].rearrange("p i k b -> p (i k) b"),
                                    ps[:, 0, 0:16 * B].rearrange("p (i b) -> p i b", b=B),
                                    mod_bias[:, :, :].rearrange("p i k -> p (i k)").unsqueeze(2).to_broadcast([P, 16, B]), ALU.add))
            for s in range(4):
                if s < 2:
                    gb = ln_g[:, s, :].unsqueeze(2).to_broadcast([P, KD, B])
                    bb = ln_b[:, s, :].unsqueeze(2).to_broadcast([P, KD, B])
                    first(dve.scalar_tensor_tensor(mod_scale[:, s], mods[:, 2 * s + 1], 1.0, gb, ALU.add, ALU.mult))
                    first(dve.scalar_tensor_tensor(mod_shift[:, s], mods[:, 2 * s + 1], 1.0, bb, ALU.add, ALU.mult))
                    first(dve.tensor_tensor(mod_shift[:, s], mod_shift[:, s], mods[:, 2 * s], ALU.add))
                else:
                    first(dve.tensor_scalar(mod_scale[:, s], mods[:, 2 * s + 1], 1.0, None, ALU.add))
                    first(dve.tensor_copy(mod_shift[:, s], mods[:, 2 * s]))
            dve.wait_ge(A_ready, 1)
            dve.tensor_scalar(A[:, :, :, :], A[:, :, :, :], -1.0, None, ALU.mult).then_inc(A_ready, 1)
            dve.wait_ge(consts_ready, 4)
            dve.wait_ge(weights_in, N_WEIGHTS)
            for d in range(2):
                for c in range(KI):
                    dve.tensor_scalar(skip_diag[:, d, c, :], ident[:, :], D_col[:, d, c:c + 1], None, ALU.mult).then_inc(mods_ready, 1)
            dve.wait_ge(x_in, 16)

            with dve.Fori(0, NBLK) as blk:
                steps = [0]

                def link(ins, before_bn=False):
                    steps[0] += 1
                    ins.then_inc(dve_step.sem, 1)
                    dve.wait_ge(dve_step.sem, dve_step.at(blk, steps[0]))
                    if before_bn:
                        dve.sem_inc(bn_turns)

                tile0 = blk * TT

                def layernorm(s):
                    for j in range(TT):
                        last = dve.bn_stats(stats[:, j, :], xs_all[:, bass.ds(tile0 + j, 1), :].rearrange("p a d -> p (a d)"))
                    link(last, before_bn=True)
                    for j in range(TT):
                        last = dve.bn_aggr(mv[:, j, :], stats[:, j, :])
                    link(last)
                    dve.tensor_scalar(mv[:, :, 1], mv[:, :, 1], EPS, None, ALU.add).then_inc(stat_ready.sem, 1)
                    dve.wait_ge(std_ready.sem, std_ready.at(blk, s + 1))
                    link(dve.reciprocal(rstd[:, :], rstd[:, :]))
                    for j in range(TT):
                        last = dve.tensor_scalar(xn[:, j, :], xs_all[:, bass.ds(tile0 + j, 1), :].rearrange("p a d -> p (a d)"),
                                                 mv[:, j, 0:1], rstd[:, j:j + 1], ALU.subtract, ALU.mult)
                    last.then_inc(xn_ready.sem, 1)

                def residual(r, bank):
                    for b in range(BB):
                        dve.wait_ge(res_mm.sem, res_mm.at(blk, BB * r + b + 1))
                        acc = ps[:, bank + b, :].rearrange("p (j d) -> p j d", d=D)
                        part = bc_rest[:, :].rearrange("p (j d) -> p j d", d=D)
                        link(dve.tensor_tensor(part, acc, gate[:, b, GATE_OF[r], :].unsqueeze(1).to_broadcast([P, QT, D]), ALU.mult))
                        xt = xs_all[:, bass.ds(tile0 + QT * b, QT), :]
                        dve.tensor_tensor(xt, xt, part, ALU.add).then_inc(res_done.sem, 1)
                        dve.wait_ge(x_in, 16)
                        dve.wait_ge(res_done.sem, res_done.at(blk, BB * r + b + 1))

                layernorm(LN_ATT)
                for m in range(KI):
                    dve.wait_ge(k_mm.sem, k_mm.at(blk, m + 1))
                    dve.tensor_copy(kT[:, m, :], ps[:, (6 + m) % 8, :]).then_inc(k_ready.sem, 1)
                for i in range(2):
                    dve.wait_ge(v_mm.sem, v_mm.at(blk, i + 1))
                    dve.tensor_copy(v[:, 2 * i:2 * i + 2, :], ps[:, 2 + i, :].rearrange("p (j d) -> p j d", d=D)).then_inc(v_ready.sem, 1)

                def row_max(g):
                    s, keys = g % 4, P * (g // GT % QT + 1)
                    dve.wait_ge(score_mm.sem, score_mm.at(blk, g + 1))
                    if g >= 4:
                        dve.wait_ge(probs_ready.sem, probs_ready.at(blk, GH * (g - 3)))
                    dve.tensor_reduce(nmax[:, s, :], ps[:, GH * (g % 2):GH * (g % 2 + 1), 0:keys], AX.X, ALU.max, negate=True).then_inc(max_ready.sem, 1)

                def take_probsT(g):
                    s, nk = g % 4, g // GT % QT + 1
                    dve.wait_ge(probsT_mm.sem, probsT_mm.at(blk, g + 1))
                    if g >= 4:
                        dve.wait_ge(pv_mm.sem, pv_mm.at(blk, g - 3))
                    dve.tensor_copy(probsT[:, s, 0:nk].rearrange("p k h q -> p (k h q)"), ps[:, 4 + g % 2, 0:nk * GH * P]).then_inc(probsT_ready.sem, 1)

                def heads_out(ti):
                    dve.wait_ge(pv_mm.sem, pv_mm.at(blk, GT * (ti + 1)))
                    link(dve.reciprocal(rsum[:, ti, :], psum_exp[:, ti, :]))
                    dve.tensor_tensor(o_sb[:, ti, :].rearrange("p (h e) -> p h e", e=HD),
                                      ps[:, 6 + ti % 2, 0:D].rearrange("p (h e) -> p h e", e=HD),
                                      rsum[:, ti, :].unsqueeze(2).to_broadcast([P, H, HD]), ALU.mult).then_inc(o_ready.sem, 1)

                dve.wait_ge(gate_in.sem, gate_in.at(blk, 16))
                row_max(0)
                for g in range(NG):
                    if g + 1 < NG:
                        row_max(g + 1)
                    take_probsT(g)
                    if g % GT == 1 and g > GT:
                        heads_out(g // GT - 1)
                heads_out(TT - 1)
                residual(RES_ATT, 2)
                layernorm(LN_MLP)
                residual(RES_MLP, 2)
                layernorm(LN_SSM)
                for d in range(2):
                    bc = ps[:, 2, :]
                    dve.wait_ge(xp_mm.sem, xp_mm.at(blk, (KI + 1) * d + 1))
                    link(dve.tensor_copy(bc_parts[:, 0, :], bc))
                    link(dve.tensor_tensor(bc_rest[:, :], bc, bc_parts[:, 0, :], ALU.subtract))
                    link(dve.tensor_copy(bc_parts[:, 1, :], bc_rest[:, :]))
                    link(dve.tensor_tensor(bc_rest[:, :], bc_rest[:, :], bc_parts[:, 1, :], ALU.subtract))
                    dve.tensor_copy(bc_parts[:, 2, :], bc_rest[:, :]).then_inc(bc_ready.sem, 1)
                    dve.wait_ge(pre_ready.sem, pre_ready.at(blk, KI * d + KI))
                    dve.scalar_tensor_tensor(kT[:, :, :], qT[:, :, :], -1.0, qT[:, :, :], ALU.mult, ALU.min).then_inc(abs_ready.sem, 1)
                    dve.wait_ge(exp_ready.sem, exp_ready.at(blk, d + 1))
                    dve.tensor_scalar(u, kT[:, :, :], 1.0, None, ALU.add).then_inc(one_ready.sem, 1)
                    dve.wait_ge(one_ready.sem, one_ready.at(blk, d + 1))
                    link(dve.scalar_tensor_tensor(kT[:, :, :], u, -1.0, kT[:, :, :], ALU.add, ALU.subtract))
                    link(dve.scalar_tensor_tensor(qT[:, :, :], qT[:, :, :], 0.0, kT[:, :, :], ALU.max, ALU.subtract))
                    dve.wait_ge(log_ready.sem, log_ready.at(blk, d + 1))
                    dve.tensor_tensor(dt[:, :, :], dt[:, :, :], qT[:, :, :], ALU.add).then_inc(dt_ready.sem, 1)
                    dve.wait_ge(dt_ready.sem, dt_ready.at(blk, d + 1))
                    dve.wait_ge(in_ready.sem, in_ready.at(blk, 2 * KI * (d + 1)))
                    dve.tensor_tensor(u, dt[:, :, :], xsT, ALU.mult).then_inc(u_ready.sem, 1)
                    edge = 0 if d == 0 else T - 1
                    dve.memset(ps[:, 0:2, :].rearrange("p a (b t) -> p a b t", t=T)[:, :, :, edge:edge + 1], 0.0).then_inc(reset_ready.sem, 1)
                    dve.wait_ge(reset_ready.sem, reset_ready.at(blk, d + 1))
                    way = slice(None) if d == 0 else slice(None, None, -1)

                    def scan_pair(r, pr, odd, ring_full=True):
                        dve.wait_ge(uB_ready.sem, uB_ready.at(r, pr + 1))
                        if ring_full:
                            dve.wait_ge(hC_ready.sem, hC_ready.at(r, pr - 3))
                        for e in range(2):
                            dve.wait_ge(dA_ready.sem, dA_ready.at(r, 2 * pr + e + 1))
                            dve.tensor_tensor_scan(hst[2 * odd + pr][:, e, :][:, way], ps[:, e, :][:, way], uB[:, pr, e, :][:, way],
                                                   0.0, ALU.mult, ALU.add).then_inc(scan_done.sem, 1)

                    def times_C(r, pr, odd):
                        dve.wait_ge(C_mm.sem, C_mm.at(r, 1))
                        dve.wait_ge(scan_done.sem, scan_done.at(r, 2 * pr + 2))
                        dve.wait_ge(y_mm.sem, y_mm.at(r, pr - 1))
                        dve.tensor_tensor(hC[:, pr], hst[2 * odd + pr], ps[:, BANK_C:BANK_C + 1, :].to_broadcast([P, 2, NB]),
                                          ALU.mult).then_inc(hC_ready.sem, 1)

                    def state(r, odd, ring_full=True):
                        scan_pair(r, 0, odd, ring_full)
                        times_C(r - 1, 1, 1 - odd)
                        scan_pair(r, 1, odd, ring_full)
                        times_C(r, 0, odd)

                    r0 = (blk * 2 + d) * NS
                    dve.wait_ge(hC_ready.sem, hC_ready.at(r0, 0))
                    scan_pair(r0, 0, 0, False)
                    scan_pair(r0, 1, 0, False)
                    times_C(r0, 0, 0)
                    state(r0 + 1, 1, False)
                    with dve.Fori(2, NS, 2) as n:
                        state(r0 + n, 0)
                        state(r0 + n + 1, 1)
                    times_C(r0 + (NS - 1), 1, 1)
                    dve.wait_ge(y_mm.sem, y_mm.at(r0 + (NS - 1), 2))
                    dve.tensor_tensor(u, ps[:, BANK_Y:BANK_Y + KI, :], szT, ALU.mult).then_inc(g_ready.sem, 1)
                    residual(RES_SSM + d, 0)
                layernorm(LN_GLU)
                for m in range(KG):
                    dve.wait_ge(glu_mm.sem, glu_mm.at(blk, KG + m + 1))
                    dve.wait_ge(glu_silu.sem, glu_silu.at(blk, m + 1))
                    dve.tensor_tensor(u[:, m, :], ps[:, (6 + m) % 8, :], inner[:, m, :], ALU.mult).then_inc(glu_ready.sem, 1)
                residual(RES_GLU, 2)
                assert steps[0] == DVE_STEPS, steps[0]

        @block.tensor
        def _(pe):
            pe.wait_ge(silu_ready, 1)
            pe.wait_ge(mods_in, N_MODS)
            pe.wait_ge(consts_ready, 4)
            of_kind = [(wada, 1, 0), (wada, 1, 1), (wada, 1, 3), (wada, 1, 4),
                       (wada1[0], 0, 0), (wada1[0], 0, 1), (wada1[1], 0, 0), (wada1[1], 0, 1)]
            for i, (w, cn, col) in enumerate(of_kind):
                for m in range(KD):
                    o = (i * KD + m) * B
                    for k in range(KD):
                        pe.matmul(ps[:, 0, o:o + B], w[:, k, col * D + m * P:col * D + (m + 1) * P], (cond_col, silu_col)[cn][:, k, :],
                                  start=(k == 0), stop=(k == KD - 1))
            for i, (w, cn, col) in enumerate(((wada, 1, 2), (wada, 1, 5), (wada1[0], 0, 2), (wada1[1], 0, 2))):
                o = ps[0:B, 1 + i // 2, (i % 2) * D:(i % 2 + 1) * D]
                for k in range(KD):
                    pe.matmul(o, (cond_col, silu_col)[cn][:, k, :], w[:, k, col * D:(col + 1) * D], start=(k == 0), stop=False)
                last = pe.matmul(o, ones_row[:, 0:B], gate_bias[:, i, :], start=False, stop=True)
            last.then_inc(mods_mm, 1)
            pe.wait_ge(rows_ready, 1)
            pe.wait_ge(weights_in, N_WEIGHTS)
            pe.wait_ge(mods_ready, 2 * KI)

            def transpose_block(src, o, blk):
                for c in range(KD):
                    for j in range(TT):
                        last = pe.transpose(ps[:, c, j * P:(j + 1) * P], src[:, j, c * P:(c + 1) * P], ident[:, :])
                    last.then_inc(o.sem, 1)

            def project(bank, lhs_of, kn, w, m):
                for k in range(kn):
                    last = pe.matmul(ps[:, bank, :], w[:, k, m * P:(m + 1) * P], lhs_of[:, k, :], start=(k == 0), stop=(k == kn - 1))
                return last

            def to_residual(bank, act_T, kn, w, bias=None):
                for b in range(BB):
                    for j in range(QT):
                        o = ps[:, bank + b, j * D:(j + 1) * D]
                        t = (b * QT + j) * P
                        if bias is not None:
                            pe.matmul(o, ones_row[:, :], bias, start=True, stop=False)
                        for k in range(kn):
                            last = pe.matmul(o, act_T[:, k, t:t + P], w[:, k, :], start=(k == 0 and bias is None), stop=(k == kn - 1))
                    last.then_inc(res_mm.sem, 1)

            with pe.Fori(0, NBLK) as blk:
                def layernorm(s):
                    pe.wait_ge(xn_ready.sem, xn_ready.at(blk, s + 1))
                    transpose_block(xn, xnT_mm, blk)
                    pe.wait_ge(hT_ready.sem, hT_ready.at(blk, KD * s + KD))

                layernorm(LN_ATT)
                for w, o, bank in ((wq, q_mm, 2), (wk, k_mm, 6)):
                    wf = w[:, :, :, :].rearrange("p k h e -> p k (h e)")
                    for m in range(KI):
                        project((bank + m) % 8, hT, KD, wf, m).then_inc(o.sem, 1)
                for j in range(TT):
                    if j % 2 == 0:
                        pe.wait_ge(q_ready.sem, q_ready.at(blk, j // 2 + 1))
                    for k in range(KD):
                        last = pe.matmul(ps[:, 2 + j // 2, (j % 2) * D:(j % 2 + 1) * D], hT[:, k, j * P:(j + 1) * P], wv[:, k, :],
                                         start=(k == 0), stop=(k == KD - 1))
                    if j % 2 == 1:
                        last.then_inc(v_mm.sem, 1)
                pe.wait_ge(q_ready.sem, q_ready.at(blk, KI))
                pe.wait_ge(k_ready.sem, k_ready.at(blk, KI))
                pe.wait_ge(v_ready.sem, v_ready.at(blk, 2))

                def scores(g):
                    ti, hg = g // GT, g % GT
                    b, qc = ti // QT, ti % QT
                    keys = P * (qc + 1)
                    if g >= 2:
                        pe.wait_ge(probs_ready.sem, probs_ready.at(blk, GH * (g - 1)))
                    for i in range(GH):
                        h = GH * hg + i
                        rows = slice(HP * (h % 4), HP * (h % 4 + 1))
                        pe.matmul(ps[:, GH * (g % 2) + i, 0:keys], qT[rows, h // 4, ti * P:(ti + 1) * P],
                                  kT[rows, h // 4, b * T:b * T + keys], start=True, stop=False)
                    for i in range(GH):
                        last = pe.matmul(ps[:, GH * (g % 2) + i, qc * P:(qc + 1) * P], ident_b[:, :], causal_b[:, :],
                                         start=False, stop=True)
                    last.then_inc(score_mm.sem, 1)

                def transpose_probs(g):
                    s, nk = g % 4, g // GT % QT + 1
                    pe.wait_ge(probs_ready.sem, probs_ready.at(blk, GH * (g + 1)))
                    if g >= 2:
                        pe.wait_ge(probsT_ready.sem, probsT_ready.at(blk, g - 1))
                    for k in range(nk):
                        for i in range(GH):
                            o = (k * GH + i) * P
                            last = pe.transpose(ps[:, 4 + g % 2, o:o + P], probs[:, s, i, k * P:(k + 1) * P], ident[:, :])
                    last.then_inc(probsT_mm.sem, 1)

                def times_v(g):
                    ti, hg, s = g // GT, g % GT, g % 4
                    b, nk = ti // QT, ti % QT + 1
                    pe.wait_ge(probsT_ready.sem, probsT_ready.at(blk, g + 1))
                    if hg == 0 and ti >= 2:
                        pe.wait_ge(o_ready.sem, o_ready.at(blk, ti - 1))
                    for i in range(GH):
                        h = GH * hg + i
                        for k in range(nk):
                            last = pe.matmul(ps[:, 6 + ti % 2, h * HD:(h + 1) * HD], probsT[:, s, k, i, :],
                                             v[:, b * QT + k, h * HD:(h + 1) * HD], start=(k == 0), stop=(k == nk - 1))
                    last.then_inc(pv_mm.sem, 1)

                scores(0)
                for g in range(NG):
                    if g + 1 < NG:
                        scores(g + 1)
                    if g >= 1:
                        times_v(g - 1)
                    transpose_probs(g)
                times_v(NG - 1)
                pe.wait_ge(o_ready.sem, o_ready.at(blk, TT))
                transpose_block(o_sb, oT_mm, blk)
                pe.wait_ge(oT_ready.sem, oT_ready.at(blk, KD))
                to_residual(2, oT, KD, wproj, bias_rows[:, 0, :])

                layernorm(LN_MLP)
                for m in range(KF):
                    project((2 + m) % 8, hT, KD, w1, m).then_inc(up_mm.sem, 1)
                pe.wait_ge(gelu_ready.sem, gelu_ready.at(blk, KF))
                to_residual(2, inner, KF, w2, bias_rows[:, 1, :])

                layernorm(LN_SSM)
                for d in range(2):
                    if d == 1:
                        pe.wait_ge(res_done.sem, res_done.at(blk, BB * (RES_SSM + 1)))
                    for m in range(2 * KI):
                        project((2 + m) % 8, hT, KD, w_in[d], m).then_inc(in_mm.sem, 1)
                    pe.wait_ge(in_ready.sem, in_ready.at(blk, 2 * KI * (d + 1)))
                    project(2, xsT, KI, w_xp[d], KI).then_inc(xp_mm.sem, 1)
                    for m in range(KI):
                        project(3 + m, xsT, KI, w_xp[d], m).then_inc(xp_mm.sem, 1)
                    pe.wait_ge(pre_ready.sem, pre_ready.at(blk, KI * (d + 1)))
                    pe.wait_ge(bc_ready.sem, bc_ready.at(blk, d + 1))
                    for c in range(KI):
                        pe.matmul(ps[:, BANK_Y + c, :], skip_diag[:, d, c, :], xsT[:, c, :], start=True, stop=False)

                    def spread(bank, row):
                        for k in range(3):
                            last = pe.matmul(ps[:, bank, :], ident_b[:, bass.ds(row, 1)].to_broadcast([P, P]), bc_parts[:, k, :],
                                             start=(k == 0), stop=(k == 2))
                        return last

                    def spread_B(r, n):
                        pe.wait_ge(B_ready.sem, B_ready.at(r, 0))
                        spread(BANK_B, n).then_inc(B_mm.sem, 1)

                    def spread_C(r, n):
                        pe.wait_ge(hC_ready.sem, hC_ready.at(r, 0))
                        spread(BANK_C, n + NS).then_inc(C_mm.sem, 1)

                    def sum_pair(r, pr, stop=False):
                        pe.wait_ge(hC_ready.sem, hC_ready.at(r, pr + 1))
                        for e in range(2):
                            last = pe.matmul(ps[:, BANK_Y + 2 * pr + e, :], ident[:, :], hC[:, pr, e, :], start=False, stop=stop)
                        last.then_inc(y_mm.sem, 1)

                    r0 = (blk * 2 + d) * NS
                    for i in range(NR):
                        spread_B(r0 + i, i)
                    spread_C(r0, 0)
                    spread_B(r0 + NR, NR)
                    sum_pair(r0, 0)
                    with pe.Fori(1, NS - NR) as n:
                        r = r0 + n
                        spread_C(r, n)
                        sum_pair(r - 1, 1)
                        spread_B(r + NR, n + NR)
                        sum_pair(r, 0)
                    for n in range(NS - NR, NS - 1):
                        spread_C(r0 + n, n)
                        sum_pair(r0 + (n - 1), 1)
                        sum_pair(r0 + n, 0)
                    rl = r0 + (NS - 1)
                    spread_C(rl, NS - 1)
                    sum_pair(rl - 1, 1)
                    sum_pair(rl, 0, True)
                    sum_pair(rl, 1, True)
                    pe.wait_ge(g_ready.sem, g_ready.at(blk, d + 1))
                    to_residual(0, u, KI, w_out[d])

                layernorm(LN_GLU)
                for w, bank in ((wg1, 2), (wg2, 6)):
                    for m in range(KG):
                        project((bank + m) % 8, hT, KD, w, m).then_inc(glu_mm.sem, 1)
                pe.wait_ge(glu_ready.sem, glu_ready.at(blk, KG))
                to_residual(2, u, KG, wg3)


_MATRICES = ['L0_cond_Wqkv', 'L0_cond_Wproj', 'L0_cond_W1', 'L0_cond_W2', 'L0_cond_Wada', 'L1_cond_adaln_mamba_w',
             'L1_cond_adaln_mlp_w', 'L1_cond_mlp_w1', 'L1_cond_mlp_w2', 'L1_cond_mlp_w3',
             'L1_cond_fwd_in_w', 'L1_cond_fwd_xproj_w', 'L1_cond_fwd_out_w',
             'L1_cond_bwd_in_w', 'L1_cond_bwd_xproj_w', 'L1_cond_bwd_out_w']


def kernel(**inputs):
    import numpy as _np
    import concourse.bacc as _bacc
    from concourse import mybir as _mybir
    from concourse.bass_utils import run_bass_kernel_spmd as _run

    get = lambda name: _np.asarray(inputs[name])
    P, D = 128, 256
    third = lambda name, i: get(name)[i * D:(i + 1) * D]
    by_channel = lambda a: a.reshape(-1, P).T
    l0, l1, mamba, glu = 'L0_cond_', 'L1_cond_', 'L1_cond_adaln_mamba_b', 'L1_cond_adaln_mlp_b'
    shifts = [third(l0 + 'bada', i) for i in (0, 1, 3, 4)] + [third(mamba, 0), third(mamba, 1), third(glu, 0), third(glu, 1)]
    cond = get('cond_1024')
    columns = _np.concatenate(
        [cond[:, k * P:(k + 1) * P].T for k in range(D // P)] + [by_channel(a) for a in shifts + [
            get(l0 + 'g1'), get(l0 + 'g2'), get(l0 + 'be1'), get(l0 + 'be2'), get(l0 + 'b1'),
            get(l1 + 'fwd_dt_bias'), get(l1 + 'bwd_dt_bias'), get(l1 + 'fwd_D'), get(l1 + 'bwd_D')]], axis=1)
    rows = _np.concatenate([third(l0 + 'bada', 2), third(l0 + 'bada', 5), third(mamba, 2), third(glu, 2),
                            get(l0 + 'bproj'), get(l0 + 'b2')])[None, :]
    A_log = _np.concatenate([get(l1 + n + 'A_log')[k * P:(k + 1) * P] for n in ('fwd_', 'bwd_') for k in range(4)], axis=1)

    nc = _bacc.Bacc("TRN2", target_bir_lowering=False, num_devices=1)
    arrays, args = {}, []
    for name, a in [('x', get('x')), ('columns', columns), ('rows', rows), ('A_log', A_log)] + [(n, get(n)) for n in _MATRICES]:
        a = _np.ascontiguousarray(a)
        arrays[f"in_{name}_dram"] = a
        args.append(nc.dram_tensor(f"in_{name}_dram", a.shape, _mybir.dt.from_np(a.dtype), kind="ExternalInput").ap())
    args.append(nc.dram_tensor("out_0_dram", get('x').shape, _mybir.dt.float32, kind="ExternalOutput").ap())
    args.append(nc.dram_tensor("gate_rows_dram", (cond.shape[0], 4 * D), _mybir.dt.float32, kind="Internal").ap())
    cond_transformer_mamba_kernel(nc, *args)
    r = _run(nc, [arrays], core_ids=[0])
    return r.results[0]["out_0_dram"]
```

```python
import numpy as np
import concourse.bass as bass
from concourse import mybir
from contextlib import ExitStack


class Flow:

    def __init__(self, sem, per, start=0):
        self.sem, self.per, self.start = sem, per, start

    def at(self, rnd, k):
        return rnd * self.per + (self.start + k)


def cond_transformer_mamba_kernel(
    nc, x, columns, rows, A_log, Wqkv, Wproj, W1, W2, Wada, wmamba, wglu, glu_w1, glu_w2, glu_w3,
    f_in, f_xproj, f_out, b_in, b_xproj, b_out, out, gate_rows,
):
    f32, bf16 = mybir.dt.float32, mybir.dt.bfloat16
    ALU, ACT, AX = mybir.AluOpType, mybir.ActivationFunctionType, mybir.AxisListType

    P = 128
    B, T, D = x.shape
    H = 16
    HD = D // H
    HP = 32
    KD = D // P
    NB = T
    NBLK = B
    TT = NB // P
    KF = W1.shape[1] // P
    DI = f_out.shape[0]
    KI = DI // P
    NS = A_log.shape[1] // (2 * KI)
    KG = glu_w1.shape[1] // P
    KQ = H * HP // P
    EPS = 1e-5
    NEG = -1e30
    NR = 4
    AHEAD = 3
    BEHIND = 2
    NU = 4
    PARTS = 3
    LN_ATT, LN_MLP, LN_SSM, LN_GLU = range(4)
    RES_ATT, RES_MLP, RES_GLU = range(3)
    GATE_SSM, GATE_GLU = 0, 1

    LIGHT, HEADS, HEAVY, LONG = 1.0, 1.5, 2.0, 2.0
    STEPS = dict(norm=5, qkv=11, heads=37, proj=4, up=11, down=9, ins=11, dts=19, post=6, glu=16)
    ROOM = dict(norm=[HEAVY, HEAVY, HEAVY, LIGHT, LIGHT], qkv=[HEAVY] * 10 + [LIGHT], heads=[HEADS] * STEPS["heads"],
                proj=[LIGHT, HEAVY, HEAVY, HEAVY], up=[HEAVY] * 8 + [LIGHT, LONG, LIGHT], down=[HEAVY] * 9,
                ins=[HEAVY] * 8 + [LIGHT, LONG, LIGHT], dts=[HEAVY] * 10 + [LIGHT] * 2 + [HEAVY] * 3 + [LONG] + [HEAVY] * 3,
                post=[HEAVY] * 5 + [LIGHT], glu=[HEAVY] * 4 + [LIGHT, LONG] + [HEAVY] * 4 + [LIGHT] + [HEAVY] * 5)
    FIRST_HALF, LAST_HALF = 4, 124

    LONG_STEPS = {("norm", 1), ("up", 9), ("ins", 9), ("dts", 15), ("glu", 5)}
    NO_PRODUCT = {(s, k) for s, ks in dict(norm=(0, 1, 2), up=(9, 10), ins=(9, 10), dts=range(10, 19), glu=(5,)).items() for k in ks}
    L0_FIRST = STEPS["norm"] + STEPS["qkv"] + STEPS["heads"]
    BANK_A, BANK_BC, BANK_Y, BANK_P = 0, 2, 4, 6

    class Plan:

        def __init__(self, d, has_prev, has_next):
            prepare, close = ["ins", "dts"], ["norm", "glu"]
            first, rest = ["norm", "qkv", "heads"], ["heads", "proj", "norm", "up", "down", "norm"]
            stages = prepare + has_prev * (["post"] + close) + has_next * first if d == 0 else ["post"] + has_next * (rest + prepare)
            self.steps = [(s, k) for s in stages for k in range(STEPS[s])]
            rooms = [ROOM[s][k] for s, k in self.steps]
            self.behind = [[] for i in range(2 * NS)]
            self.ahead = {}
            self.scanned = {}
            self.bank = [BANK_A + i % 2 for i in range(2 * NS)]
            pending = None
            for j, step in enumerate(self.steps):
                i = max(FIRST_HALF, FIRST_HALF - -sum(rooms[:j]) * (LAST_HALF - FIRST_HALF) // sum(rooms))
                i = int(i)
                self.behind[i].append(j)
                if pending is not None and step not in NO_PRODUCT:
                    self.scanned[j], pending = pending, None
                if step in LONG_STEPS and i + 2 < 2 * NS - 2 and self.bank[i + 1] < BANK_P:
                    self.ahead[j] = [i + 1, i + 2]
                    self.bank[i + 1], self.bank[i + 2] = BANK_P, BANK_P + 1
                    pending = i + 2
            self.before = [max([k for k in range(i) if self.bank[k] == self.bank[i]], default=i - 2 if self.bank[i] < BANK_P else None)
                           for i in range(2 * NS)]

    def interleave(state, steps, plan, before=None):
        for i in range(2 * NS):
            state(i // 2, i % 2)
            for j in plan.behind[i]:
                if before:
                    before(j)
                next(steps)
        assert next(steps, None) is None

    x_tiles = x.rearrange("b (h p) d -> p (b h) d", p=P)
    out_tiles = out.rearrange("b (h p) d -> p (b h) d", p=P)

    ctx = ExitStack()
    with ctx:
        def sb(name, shape, dt=f32):
            return ctx.enter_context(nc.sbuf_tensor(name, shape, dt))

        def sem(name):
            return ctx.enter_context(nc.semaphore(name))

        def flow(name, per=1, start=0):
            return Flow(sem(name), per, start)

        wq = sb("wq", [P, KD, H, HP])
        wk = sb("wk", [P, KD, H, HP])
        wv = sb("wv", [P, KD, D])
        wproj = sb("wproj", [P, KD, D])
        w1 = sb("w1", [P, KD, KF * P])
        w2 = sb("w2", [P, KF, D])
        w_in = [sb(f"w_in{d}", [P, KD, 2 * DI]) for d in range(2)]
        w_xp = [sb(f"w_xp{d}", [P, KI, DI + 2 * NS]) for d in range(2)]
        w_out = [sb(f"w_out{d}", [P, KI, D]) for d in range(2)]
        wg1 = sb("wg1", [P, KD, KG * P])
        wg2 = sb("wg2", [P, KD, KG * P])
        wg3 = sb("wg3", [P, KG, D])
        bias_rows = sb("bias_rows", [1, 2, D])
        col_in = sb("col_in", [P, columns.shape[1]])
        cols = [0]

        def column(*shape):
            at, n = cols[0], int(np.prod(shape))
            cols[0] += n
            part = col_in[:, at:at + n]
            return part if len(shape) == 1 else part.rearrange("p (a b) -> p a b", b=shape[1])

        cond_col = column(KD, B)
        mod_bias = column(8, KD)
        ln_g, ln_b = column(2, KD), column(2, KD)
        b1_col = column(KF)
        dtb_col, D_col = column(2, KI), column(2, KI)
        A = sb("A", [P, 2, KI, NS])
        ident = sb("ident", [P, P])
        ident_b = sb("ident_b", [P, P], bf16)
        causal_b = sb("causal_b", [P, P], bf16)
        pick = sb("pick", [P, HP], bf16)
        ones_row = sb("ones_row", [1, P])
        zeros = sb("zeros", [P, 2])
        skip_diag = sb("skip_diag", [P, 2, KI, P])
        silu_col = sb("silu_col", [P, KD, B])
        mods = sb("mods", [P, 8, KD, B])
        mod_scale = sb("mod_scale", [P, 4, KD, B])
        mod_shift = sb("mod_shift", [P, 4, KD, B])
        gate_l0 = sb("gate_l0", [P, 2, D])
        gate_l1 = sb("gate_l1", [P, 2, D])
        xs_all = sb("xs_all", [P, NBLK * TT, D])
        xn = sb("xn", [P, TT, D])
        hT = sb("hT", [P, KD, NB])
        hT_ssm = sb("hT_ssm", [P, KD, NB])
        stats = sb("stats", [P, TT, 6])
        mv = sb("mv", [P, TT, 2])
        rstd = sb("rstd", [P, TT])
        qk = sb("qk", [P, 2 * KQ, NB])
        qT, kT = qk[:, 0:KQ, :], qk[:, KQ:2 * KQ, :]
        v = sb("v", [P, TT, D])
        probs = sb("probs", [P, 2, T])
        probsT = sb("probsT", [P, TT * 2 * P])
        o_sb = sb("o_sb", [P, TT, D])
        prime = sb("prime", [P, 6])
        nmax = sb("nmax", [P, 2])
        psum_exp = sb("psum_exp", [P, TT, H])
        rsum = sb("rsum", [P, TT, H])
        xsT = sb("xsT", [P, KI, NB])
        szT = sb("szT", [P, 2, KI, NB])
        dt = sb("dt", [P, 2, KI, NB])
        u = sb("u", [P, 2, KI, NB])
        bc_parts = sb("bc_parts", [P, PARTS, NB], bf16)
        bc_rows = sb("bc_rows", [PARTS * HP, 2, 4, NB], bf16)
        gT = sb("gT", [P, KI, NB])
        B_sb = sb("B_sb", [P, NR, NB])
        uB = sb("uB", [P, NU, 2, NB])
        hst = sb("hst", [P, NR, KI, NB])

        part = xn
        bc_rest = probs[:, 0, :]
        oT = v
        hidden = qk
        pre, expo = qT, kT
        flat = lambda t, n: t.rearrange("p a b -> p (a b)")[:, 0:KD * n].rearrange("p (k n) -> p k n", k=KD)
        wada = flat(hst[:, :, :, :].rearrange("p r k n -> p r (k n)"), 6 * D)
        wada1 = [flat(uB[:, :, :, :].rearrange("p r k n -> p r (k n)"), 3 * D), flat(qk[:, :, :], 3 * D)]
        mod_rows = gT[0:B, :, :].rearrange("p a b -> p (a b)")
        gate_bias = B_sb[0:1, :, :]

        ps = ctx.enter_context(nc.psum_tensor("ps", [P, 8, 2 * NB], f32))

        mods_in, x_in, weights_in, rows_out, out_done = map(sem, ("mods_in", "x_in", "weights_in", "rows_out", "out_done"))
        pads_zero, pool_step, consts_ready, silu_ready, A_ready, mods_mm = map(
            sem, ("pads_zero", "pool_step", "consts_ready", "silu_ready", "A_ready", "mods_mm"))
        dve_setup, rows_ready, mods_ready, bn_turns = map(sem, ("dve_setup", "rows_ready", "mods_ready", "bn_turns"))
        gate0_in, gate1_in = flow("gate0_in", 16), flow("gate1_in", 16)
        norm_step = [flow(f"norm_step{s}", 3) for s in range(4)]
        stat_ready = [flow(f"stat_ready{s}") for s in range(4)]
        std_ready = [flow(f"std_ready{s}") for s in range(4)]
        xn_ready = [flow(f"xn_ready{s}") for s in range(4)]
        xnT_mm = [flow(f"xnT_mm{s}") for s in range(4)]
        hT_ready = [flow(f"hT_ready{s}") for s in range(4)]
        qkv_mm, q_ready, kv_ready = flow("qkv_mm", 10), flow("q_ready", 4), flow("kv_ready", 6)
        NG = TT * H // 2
        score_mm, max_ready, probs_ready = flow("score_mm", NG), flow("max_ready", NG), flow("probs_ready", 2 * NG)
        probsT_mm, probsT_ready, pv_mm, o_raw = flow("probsT_mm", NG), flow("probsT_ready", NG), flow("pv_mm", NG), flow("o_raw", NG)
        rsum_ready, o_ready, oT_mm, oT_ready = flow("rsum_ready", TT), flow("o_ready", TT), flow("oT_mm"), flow("oT_ready")
        up_mm, up_ready, gelu_ready = flow("up_mm", KF), flow("up_ready", KF), flow("gelu_ready")
        glu_mm, glu_raw, glu_silu, glu_ready = flow("glu_mm", 2 * KG), flow("glu_raw", KG), flow("glu_silu"), flow("glu_ready", KG)
        res_mm, res_part, res_done = ([flow(f"{n}{r}") for r in range(3)] for n in ("res_mm", "res_part", "res_done"))
        post_mm, post_part, post_done = flow("post_mm"), flow("post_part"), flow("post_done")
        in_mm, in_raw, in_ready = flow("in_mm", 2 * KI), flow("in_raw", 2 * KI), flow("in_ready", 2)
        bc_mm, bc_step, bc_ready, bc_in = flow("bc_mm"), flow("bc_step", 4), flow("bc_ready"), flow("bc_in", 16 * PARTS * 4)
        dt_mm, pre_ready, abs_ready, exp_ready, one_ready, log_ready = (
            flow("dt_mm", KI), flow("pre_ready", KI), flow("abs_ready"), flow("exp_ready"), flow("one_ready"), flow("log_ready"))
        soft_step, dt_ready, u_ready, g_ready = flow("soft_step", 2), flow("dt_ready"), flow("u_ready"), flow("g_ready", 1, 1)
        BC_mm, B_ready = flow("BC_mm"), flow("B_ready", 1, 2)
        dA_ready, uB_ready = flow("dA_ready", 2), flow("uB_ready", 2, 2 * NR)
        scan_done, hC_ready, y_mm = flow("scan_done", 2, 4), flow("hC_ready", 2, 2 * NR), flow("y_mm", 1, NR)

        block = ctx.enter_context(nc.Block())

        @block.sync
        def _(sp):
            sp.dma_start(col_in[:, :], columns).then_inc(mods_in, 16)
            sp.dma_start(gate_bias, rows[:, 0:4 * D].rearrange("a (i n) -> a i n", n=D)).then_inc(mods_in, 16)
            sp.dma_start(wada, Wada.rearrange("(k p) n -> p k n", p=P)).then_inc(mods_in, 16)
            sp.dma_start(wada1[0], wmamba.rearrange("(k p) n -> p k n", p=P)).then_inc(mods_in, 16)
            sp.dma_start(wada1[1], wglu.rearrange("(k p) n -> p k n", p=P)).then_inc(mods_in, 16)
            sp.dma_start(xs_all[:, :, :], x_tiles).then_inc(x_in, 16)
            sp.wait_ge(pads_zero, 2)
            for w, c in ((wq, 0), (wk, 1)):
                for k in range(KD):
                    sp.dma_start(w[:, k, :, 0:HD], Wqkv[k * P:(k + 1) * P, c * D:(c + 1) * D]
                                 .rearrange("p (h e) -> p h e", e=HD)).then_inc(weights_in, 16)
            sp.dma_start(wv[:, :, :], Wqkv[:, 2 * D:3 * D].rearrange("(k p) n -> p k n", p=P)).then_inc(weights_in, 16)
            loads = [(wproj, Wproj), (w1, W1), (w2, W2), (w_in[0], f_in), (w_in[1], b_in), (w_xp[0], f_xproj),
                     (w_xp[1], b_xproj), (w_out[0], f_out), (w_out[1], b_out), (wg1, glu_w1), (wg2, glu_w2), (wg3, glu_w3)]
            for w, src in loads:
                sp.dma_start(w[:, :, :], src.rearrange("(k p) n -> p k n", p=P)).then_inc(weights_in, 16)
            sp.dma_start(A[:, :, :, :].rearrange("p d k n -> p (d k n)"), A_log).then_inc(weights_in, 16)
            sp.dma_start(bias_rows[:, :, :].rearrange("a i n -> a (i n)"), rows[:, 4 * D:6 * D]).then_inc(weights_in, 16)
            sp.wait_ge(rows_ready, 1)
            sp.dma_start(gate_rows, mod_rows).then_inc(rows_out, 16)
            sp.wait_ge(rows_out, 16)

            def load_gates(gates, o, b, half):
                sp.dma_start(gates[:, :, :].rearrange("p g d -> p (g d)"),
                             gate_rows[bass.ds(b, 1), half * 2 * D:(half + 1) * 2 * D].rearrange("a n -> (a n)")
                             .partition_broadcast(P)).then_inc(o.sem, 16)

            def stack_rows(p, d):
                sp.wait_ge(bc_ready.sem, bc_ready.at(p, 1))
                for q in range(4):
                    for k in range(PARTS):
                        sp.dma_start(bc_rows[k * HP:(k + 1) * HP, d, q, :], bc_parts[q * HP:(q + 1) * HP, k, :]).then_inc(bc_in.sem, 16)

            def store(b):
                sp.wait_ge(res_done[RES_GLU].sem, res_done[RES_GLU].at(b, 1))
                sp.dma_start(out_tiles[:, bass.ds(b * TT, TT), :], xs_all[:, bass.ds(b * TT, TT), :]).then_inc(out_done, 16)

            def period(b, has_prev, has_next):
                if has_next:
                    sp.wait_ge(res_done[RES_MLP].sem, res_done[RES_MLP].at(b, 1))
                    load_gates(gate_l0, gate0_in, b + 1, 0)
                stack_rows(2 * b + 1, 1)
                if has_prev:
                    store(b - 1)
                    load_gates(gate_l1, gate1_in, b, 1)
                if has_next:
                    stack_rows(2 * b + 2, 0)

            load_gates(gate_l0, gate0_in, 0, 0)
            load_gates(gate_l1, gate1_in, 0, 1)
            stack_rows(0, 0)
            period(0, False, True)
            with sp.Fori(1, NBLK - 1) as b:
                period(b, True, True)
            period(NBLK - 1, True, False)
            store(NBLK - 1)
            sp.wait_ge(out_done, 16 * NBLK)

        N_MODS, N_WEIGHTS = 16 * 5, 16 * (5 + 12 + 2)

        @block.gpsimd
        def _(pool):
            pool.memset(wq[:, :, :, :], 0.0).then_inc(pads_zero, 1)
            pool.memset(wk[:, :, :, :], 0.0).then_inc(pads_zero, 1)
            pool.memset(ident[:, :], 0.0).then_inc(pool_step, 1)
            pool.memset(causal_b[:, :], 0.0).then_inc(pool_step, 1)
            pool.memset(pick[:, :], 0.0).then_inc(pool_step, 1)
            pool.wait_ge(pool_step, 3)
            pool.affine_select(out=ident[:, :], in_=ident[:, :], compare_op=ALU.not_equal, fill=1.0, base=0,
                               pattern=[[-1, P]], channel_multiplier=1).then_inc(consts_ready, 1)
            pool.affine_select(out=causal_b[:, :], in_=causal_b[:, :], compare_op=ALU.is_ge, fill=NEG, base=0,
                               pattern=[[-1, P]], channel_multiplier=1).then_inc(consts_ready, 1)
            for k in range(PARTS):
                pool.affine_select(out=pick[:, :], in_=pick[:, :], compare_op=ALU.not_equal, fill=1.0, base=-k * HP,
                                   pattern=[[-1, HP]], channel_multiplier=1).then_inc(pool_step, 1)
                pool.wait_ge(pool_step, 4 + k)
            pool.memset(ones_row[:, :], 1.0).then_inc(consts_ready, 1)
            pool.memset(zeros[:, :], 0.0).then_inc(consts_ready, 1)
            pool.wait_ge(consts_ready, 4)
            pool.tensor_copy(ident_b[:, :], ident[:, :]).then_inc(consts_ready, 1)

            def products(p, d, n, i):
                r = p * NS + n
                pool.wait_ge(B_ready.sem, B_ready.at(r, 1))
                for e in range(2):
                    pool.wait_ge(scan_done.sem, scan_done.at(r, e + 1 - NU))
                    pool.tensor_tensor(uB[:, (2 * i + e) % NU], u[:, d, 2 * e:2 * e + 2, :],
                                       B_sb[:, i:i + 1, :].to_broadcast([P, 2, NB]), ALU.mult).then_inc(uB_ready.sem, 1)

            with pool.Fori(0, NBLK) as b:
                for d in range(2):
                    p = b * 2 + d
                    pool.wait_ge(u_ready.sem, u_ready.at(p, 1))
                    for i in range(NR):
                        products(p, d, i, i)
                    with pool.Fori(NR, NS, NR) as n0:
                        for i in range(NR):
                            products(p, d, n0 + i, i)

        @block.scalar
        def _(act):
            act.wait_ge(mods_in, N_MODS)
            act.activation(silu_col[:, :, :], cond_col, ACT.Silu).then_inc(silu_ready, 1)
            act.wait_ge(weights_in, N_WEIGHTS)
            act.activation(A[:, :, :, :], A[:, :, :, :], ACT.Exp).then_inc(A_ready, 1)
            act.activation(prime[:, 0:1], col_in[:, 0:1], ACT.Copy).then_inc(B_ready.sem, B_ready.start)
            act.wait_ge(A_ready, 2)
            act.wait_ge(mods_ready, 1)
            act.wait_ge(consts_ready, 5)

            ahead = []

            def run_ahead():
                while ahead:
                    ahead.pop(0)()

            def norm(b, s, dst):
                for i in range(STEPS["norm"]):
                    if i == 1:
                        act.wait_ge(norm_step[s].sem, norm_step[s].at(b, 1))
                        run_ahead()
                        act.wait_ge(stat_ready[s].sem, stat_ready[s].at(b, 1))
                        act.activation(rstd[:, :], mv[:, :, 1], ACT.Sqrt).then_inc(std_ready[s].sem, 1)
                    if i == 4:
                        act.wait_ge(xnT_mm[s].sem, xnT_mm[s].at(b, 1))
                        for c in range(KD):
                            col = bass.ds(b, 1)
                            last = act.activation(dst[:, c, :], ps[:, BANK_P, c * NB:(c + 1) * NB], ACT.Identity,
                                                  bias=mod_shift[:, s, c, col], scale=mod_scale[:, s, c, col])
                        last.then_inc(hT_ready[s].sem, 1)
                    yield

            def qkv(b):
                for i in range(STEPS["qkv"]):
                    if 1 <= i < 1 + KQ:
                        m = i - 1
                        act.wait_ge(qkv_mm.sem, qkv_mm.at(b, m + 1))
                        act.activation(qT[:, m, :], ps[:, BANK_P + m % 2, 0:NB], ACT.Copy, scale=float(HD) ** -0.5).then_inc(q_ready.sem, 1)
                    yield

            def heads(b, ti):
                keys = P * (ti + 1)
                for i in range(STEPS["heads"]):
                    if i % 4 == 2 and i // 4 < H // 2:
                        j = i // 4
                        g = ti * H // 2 + j
                        act.wait_ge(max_ready.sem, max_ready.at(b, g + 1))
                        if g >= 1:
                            act.wait_ge(probsT_mm.sem, probsT_mm.at(b, g))
                        for e in range(2):
                            h = j // 4 * 8 + e * 4 + j % 4
                            act.activation(probs[:, e, 0:keys], ps[:, BANK_P + g % 2, e * T:e * T + keys], ACT.Exp, bias=nmax[:, e:e + 1],
                                           accum_out=psum_exp[:, ti, h:h + 1]).then_inc(probs_ready.sem, 1)
                    yield

            def idle(n):
                for i in range(n):
                    yield

            def up(b):
                for i in range(STEPS["up"]):
                    if 1 <= i < 1 + KF:
                        m = i - 1
                        act.wait_ge(up_mm.sem, up_mm.at(b, m + 1))
                        act.activation(hidden[:, m, :], ps[:, BANK_P + m % 2, 0:NB], ACT.Identity, bias=b1_col[:, m:m + 1]).then_inc(up_ready.sem, 1)
                    if i == 1 + KF:
                        act.wait_ge(up_ready.sem, up_ready.at(b, KF))
                        run_ahead()
                        act.activation(hidden[:, :, :], hidden[:, :, :], ACT.Gelu).then_inc(gelu_ready.sem, 1)
                    yield

            def prepare(p, d):
                for i in range(STEPS["ins"]):
                    if 1 <= i < 1 + 2 * KI:
                        m = i - 1
                        dst = xsT[:, m, :] if m < KI else szT[:, d, m - KI, :]
                        act.wait_ge(in_mm.sem, in_mm.at(p, m + 1))
                        act.activation(dst, ps[:, BANK_P + m % 2, 0:NB], ACT.Copy).then_inc(in_raw.sem, 1)
                    if i == 1 + 2 * KI:
                        act.wait_ge(in_raw.sem, in_raw.at(p, 2 * KI))
                        run_ahead()
                        act.activation(xsT[:, :, :], xsT[:, :, :], ACT.Silu).then_inc(in_ready.sem, 1)
                        act.activation(szT[:, d], szT[:, d], ACT.Silu).then_inc(in_ready.sem, 1)
                    yield
                for i in range(STEPS["dts"]):
                    if i % 2 == 1 and 5 <= i < 5 + 2 * KI:
                        m = (i - 5) // 2
                        act.wait_ge(dt_mm.sem, dt_mm.at(p, m + 1))
                        act.activation(pre[:, m, :], ps[:, BANK_P + (m + 1) % 2, 0:NB], ACT.Identity,
                                       bias=dtb_col[:, d, m:m + 1]).then_inc(pre_ready.sem, 1)
                    if i == 13:
                        act.wait_ge(abs_ready.sem, abs_ready.at(p, 1))
                        act.activation(expo, expo, ACT.Exp).then_inc(exp_ready.sem, 1)
                    if i == 15:
                        act.wait_ge(pre_ready.sem, pre_ready.at(p, KI))
                        run_ahead()
                        act.wait_ge(one_ready.sem, one_ready.at(p, 1))
                        act.activation(dt[:, d], u[:, d], ACT.Ln).then_inc(log_ready.sem, 1)
                    yield

            def glu(b):
                for i in range(STEPS["glu"]):
                    if 1 <= i < 1 + KG:
                        m = i - 1
                        act.wait_ge(glu_mm.sem, glu_mm.at(b, m + 1))
                        act.activation(hidden[:, m, :], ps[:, BANK_P + m % 2, 0:NB], ACT.Copy).then_inc(glu_raw.sem, 1)
                    if i == 1 + KG:
                        act.wait_ge(glu_raw.sem, glu_raw.at(b, KG))
                        run_ahead()
                        act.activation(hidden[:, 0:KG, :], hidden[:, 0:KG, :], ACT.Silu).then_inc(glu_silu.sem, 1)
                    yield

            def layer0(b):
                yield from norm(b, LN_ATT, hT)
                yield from qkv(b)
                yield from heads(b, 0)
                yield from heads(b, 1)
                yield from idle(STEPS["proj"])
                yield from norm(b, LN_MLP, hT)
                yield from up(b)
                yield from idle(STEPS["down"])
                yield from norm(b, LN_SSM, hT_ssm)

            def close(b):
                yield from norm(b, LN_GLU, hT)
                yield from glu(b)

            def take_B(r, i):
                act.wait_ge(BC_mm.sem, BC_mm.at(r, 1))
                act.wait_ge(uB_ready.sem, uB_ready.at(r, 2 - 2 * NR))
                act.activation(B_sb[:, i % NR, :], ps[:, BANK_BC + (i + 1) % 2, 0:NB], ACT.Copy).then_inc(B_ready.sem, 1)

            def scan_pass(p, d, last, steps, plan):
                lo, hi = (1, NB) if d == 0 else (0, NB - 1)
                edge = 0 if d == 0 else NB - 1
                taken = set()

                def decays(i):
                    n, e = i // 2, i % 2
                    bank = ps[:, plan.bank[i], :]
                    if plan.before[i] is not None:
                        act.wait_ge(scan_done.sem, scan_done.at(p * NS + n, e + 1 - (i - plan.before[i])))
                    if i < 2 or plan.bank[i] >= BANK_P:
                        act.activation(bank.rearrange("p (k t) -> p k t", t=NB)[:, :, edge], zeros[:, :], ACT.Copy)
                    for c in range(2 * e, 2 * e + 2):
                        o = c % 2 * NB
                        done = act.activation(bank[:, o + lo:o + hi], dt[:, d, c, lo:hi], ACT.Exp, scale=A[:, d, c, n:n + 1])
                    done.then_inc(dA_ready.sem, 1)

                def state(n, e):
                    if n == 0 and e == 0:
                        act.wait_ge(u_ready.sem, u_ready.at(p, 1))
                    if e == 0 and n not in taken and not (last and n + AHEAD - 1 >= NS):
                        take_B(p * NS + n + AHEAD - 1, n + AHEAD - 1)
                    if plan.bank[2 * n + e] < BANK_P:
                        decays(2 * n + e)

                def before(j):
                    if j in plan.ahead:
                        ahead.extend((lambda i=i: decays(i)) for i in plan.ahead[j])
                        n = (plan.ahead[j][0] - 1) // 2 + 1
                        if not (last and n + AHEAD - 1 >= NS):
                            taken.add(n)
                            ahead.append(lambda n=n: take_B(p * NS + n + AHEAD - 1, n + AHEAD - 1))

                interleave(state, steps, plan, before)

            def period(b, has_prev, has_next):
                l0 = layer0(b + 1) if has_next else None

                def forward():
                    yield from prepare(2 * b + 1, 1)
                    if has_prev:
                        yield from idle(STEPS["post"])
                        yield from close(b - 1)
                    if has_next:
                        for i in range(L0_FIRST):
                            next(l0)
                            yield

                def backward():
                    yield from idle(STEPS["post"])
                    if has_next:
                        yield from l0
                        yield from prepare(2 * b + 2, 0)

                scan_pass(2 * b, 0, False, forward(), Plan(0, has_prev, has_next))
                scan_pass(2 * b + 1, 1, not has_next, backward(), Plan(1, has_prev, has_next))

            for _ in layer0(0):
                pass
            for _ in prepare(0, 0):
                pass
            for i in range(AHEAD - 1):
                take_B(i, i)
            period(0, False, True)
            with act.Fori(1, NBLK - 1) as b:
                period(b, True, True)
            period(NBLK - 1, True, False)
            for _ in close(NBLK - 1):
                pass

        @block.vector
        def _(dve):
            setup = [0]

            def first(ins):
                setup[0] += 1
                ins.then_inc(dve_setup, 1)
                dve.wait_ge(dve_setup, setup[0])

            dve.memset(prime[:, 1:2], 0.0).then_inc(scan_done.sem, scan_done.start)
            dve.memset(prime[:, 2:3], 0.0).then_inc(hC_ready.sem, hC_ready.start)
            dve.memset(prime[:, 3:4], 0.0).then_inc(y_mm.sem, y_mm.start)
            dve.memset(prime[:, 4:5], 0.0).then_inc(uB_ready.sem, uB_ready.start)
            dve.memset(prime[:, 5:6], 0.0).then_inc(g_ready.sem, g_ready.start)
            dve.wait_ge(mods_mm, 1)
            dve.wait_ge(mods_in, N_MODS)
            dve.tensor_copy(mod_rows, ps[0:B, 1:3, :].rearrange("p a n -> p (a n)")).then_inc(rows_ready, 1)
            first(dve.tensor_tensor(mods[:, :, :, :].rearrange("p i k b -> p (i k) b"),
                                    ps[:, 0, 0:16 * B].rearrange("p (i b) -> p i b", b=B),
                                    mod_bias.rearrange("p i k -> p (i k)").unsqueeze(2).to_broadcast([P, 16, B]), ALU.add))
            for s in range(4):
                if s < 2:
                    gb = ln_g[:, s, :].unsqueeze(2).to_broadcast([P, KD, B])
                    bb = ln_b[:, s, :].unsqueeze(2).to_broadcast([P, KD, B])
                    first(dve.scalar_tensor_tensor(mod_scale[:, s], mods[:, 2 * s + 1], 1.0, gb, ALU.add, ALU.mult))
                    first(dve.scalar_tensor_tensor(mod_shift[:, s], mods[:, 2 * s + 1], 1.0, bb, ALU.add, ALU.mult))
                    first(dve.tensor_tensor(mod_shift[:, s], mod_shift[:, s], mods[:, 2 * s], ALU.add))
                else:
                    first(dve.tensor_scalar(mod_scale[:, s], mods[:, 2 * s + 1], 1.0, None, ALU.add))
                    first(dve.tensor_copy(mod_shift[:, s], mods[:, 2 * s]))
            dve.wait_ge(A_ready, 1)
            dve.tensor_scalar(A[:, :, :, :], A[:, :, :, :], -1.0, None, ALU.mult).then_inc(A_ready, 1)
            dve.wait_ge(consts_ready, 5)
            dve.wait_ge(weights_in, N_WEIGHTS)
            for d in range(2):
                for c in range(KI):
                    dve.tensor_scalar(skip_diag[:, d, c, :], ident[:, :], D_col[:, d, c:c + 1], None, ALU.mult).then_inc(mods_ready, 1)
            dve.wait_ge(x_in, 16)

            def x_tile(b, j):
                return xs_all[:, bass.ds(b * TT + j, 1), :].rearrange("p a d -> p (a d)")

            def norm(b, s, before):
                for i in range(STEPS["norm"]):
                    if i == 0:
                        dve.wait_ge(x_in, 16)
                        if before is not None:
                            dve.wait_ge(before[0].sem, before[0].at(before[1], 1))
                        for j in range(TT):
                            last = dve.bn_stats(stats[:, j, :], x_tile(b, j))
                        last.then_inc(norm_step[s].sem, 1)
                        dve.wait_ge(norm_step[s].sem, norm_step[s].at(b, 1))
                        dve.sem_inc(bn_turns)
                        for j in range(TT):
                            last = dve.bn_aggr(mv[:, j, :], stats[:, j, :])
                        last.then_inc(norm_step[s].sem, 1)
                        dve.wait_ge(norm_step[s].sem, norm_step[s].at(b, 2))
                        dve.tensor_scalar(mv[:, :, 1], mv[:, :, 1], EPS, None, ALU.add).then_inc(stat_ready[s].sem, 1)
                    if i == 2:
                        dve.wait_ge(std_ready[s].sem, std_ready[s].at(b, 1))
                        dve.reciprocal(rstd[:, :], rstd[:, :]).then_inc(norm_step[s].sem, 1)
                        dve.wait_ge(norm_step[s].sem, norm_step[s].at(b, 3))
                        for j in range(TT):
                            last = dve.tensor_scalar(xn[:, j, :], x_tile(b, j), mv[:, j, 0:1], rstd[:, j:j + 1], ALU.subtract, ALU.mult)
                        last.then_inc(xn_ready[s].sem, 1)
                    yield

            def residual(b, bank, rnd, gates, which, gate_in, mm, mul, done):
                dve.wait_ge(gate_in.sem, gate_in.at(b, 16))
                dve.wait_ge(mm.sem, mm.at(rnd, 1))
                dve.tensor_tensor(part[:, :, :], ps[:, bank, :].rearrange("p (j d) -> p j d", d=D),
                                  gates[:, which:which + 1, :].to_broadcast([P, TT, D]), ALU.mult).then_inc(mul.sem, 1)
                dve.wait_ge(mul.sem, mul.at(rnd, 1))
                xt = xs_all[:, bass.ds(b * TT, TT), :]
                dve.tensor_tensor(xt, xt, part[:, :, :], ALU.add).then_inc(done.sem, 1)

            def qkv(b):
                for i in range(STEPS["qkv"]):
                    m = i - 1
                    if KQ <= m < 2 * KQ:
                        dve.wait_ge(qkv_mm.sem, qkv_mm.at(b, m + 1))
                        dve.tensor_copy(kT[:, m - KQ, :], ps[:, BANK_P + m % 2, 0:NB]).then_inc(kv_ready.sem, 1)
                    if 2 * KQ <= m < 2 * KQ + TT:
                        dve.wait_ge(qkv_mm.sem, qkv_mm.at(b, m + 1))
                        dve.tensor_copy(v[:, m - 2 * KQ, :], ps[:, BANK_P + m % 2, 0:D]).then_inc(kv_ready.sem, 1)
                    yield

            def heads(b, ti):
                keys, nk = P * (ti + 1), ti + 1
                for i in range(STEPS["heads"]):
                    if i % 4 == 3 and 1 <= i // 4 < 1 + H // 2:
                        j = i // 4 - 1
                        g = ti * H // 2 + j
                        h = j // 4 * 8 + j % 4
                        dve.wait_ge(pv_mm.sem, pv_mm.at(b, g + 1))
                        dve.tensor_copy(o_sb[:, ti, :].rearrange("p (a c e) -> p a c e", c=4, e=HD)[:, 2 * (j // 4):2 * (j // 4) + 2, j % 4, :],
                                        ps[:, BANK_P + g % 2, 0:2 * HD].rearrange("p (a e) -> p a e", e=HD)).then_inc(o_raw.sem, 1)
                    if i % 4 == 0 and 1 <= i // 4 < 1 + H // 2:
                        g = ti * H // 2 + i // 4 - 1
                        dve.wait_ge(probsT_mm.sem, probsT_mm.at(b, g + 1))
                        if g >= 1:
                            dve.wait_ge(pv_mm.sem, pv_mm.at(b, g))
                        dve.tensor_copy(probsT[:, 0:nk * 2 * P], ps[:, BANK_P + g % 2, 0:nk * 2 * P]).then_inc(probsT_ready.sem, 1)
                    if i % 4 == 1 and i // 4 < H // 2:
                        g = ti * H // 2 + i // 4
                        dve.wait_ge(score_mm.sem, score_mm.at(b, g + 1))
                        if g >= 1:
                            dve.wait_ge(probs_ready.sem, probs_ready.at(b, 2 * g))
                        dve.tensor_reduce(nmax[:, :], ps[:, BANK_P + g % 2, :].rearrange("p (e t) -> p e t", t=T)[:, :, 0:keys],
                                          AX.X, ALU.max, negate=True).then_inc(max_ready.sem, 1)
                    if i == STEPS["heads"] - 1:
                        dve.wait_ge(probs_ready.sem, probs_ready.at(b, (ti + 1) * H))
                        dve.reciprocal(rsum[:, ti, :], psum_exp[:, ti, :]).then_inc(rsum_ready.sem, 1)
                        dve.wait_ge(rsum_ready.sem, rsum_ready.at(b, ti + 1))
                        dve.wait_ge(o_raw.sem, o_raw.at(b, (ti + 1) * H // 2))
                        o = o_sb[:, ti, :].rearrange("p (h e) -> p h e", e=HD)
                        dve.tensor_tensor(o, o, rsum[:, ti, :].unsqueeze(2).to_broadcast([P, H, HD]), ALU.mult).then_inc(o_ready.sem, 1)
                    yield

            def project(b):
                for i in range(STEPS["proj"]):
                    if i == 1:
                        dve.wait_ge(oT_mm.sem, oT_mm.at(b, 1))
                        dve.tensor_copy(oT[:, :, :].rearrange("p a n -> p (a n)"), ps[:, BANK_P, :]).then_inc(oT_ready.sem, 1)
                    if i == 3:
                        residual(b, BANK_P + 1, b, gate_l0, 0, gate0_in, res_mm[RES_ATT], res_part[RES_ATT], res_done[RES_ATT])
                    yield

            def idle(n):
                for i in range(n):
                    yield

            def down(b):
                for i in range(STEPS["down"]):
                    if i == STEPS["down"] - 1:
                        residual(b, BANK_P, b, gate_l0, 1, gate0_in, res_mm[RES_MLP], res_part[RES_MLP], res_done[RES_MLP])
                    yield

            def prepare(p, d):
                yield from idle(STEPS["ins"])
                for i in range(STEPS["dts"]):
                    bc = ps[:, BANK_P, 0:NB]
                    if i == 2:
                        dve.wait_ge(bc_mm.sem, bc_mm.at(p, 1))
                        dve.tensor_copy(bc_parts[:, 0, :], bc).then_inc(bc_step.sem, 1)
                        dve.wait_ge(bc_step.sem, bc_step.at(p, 1))
                        dve.tensor_tensor(bc_rest, bc, bc_parts[:, 0, :], ALU.subtract).then_inc(bc_step.sem, 1)
                    if i == 3:
                        dve.wait_ge(bc_step.sem, bc_step.at(p, 2))
                        dve.tensor_copy(bc_parts[:, 1, :], bc_rest).then_inc(bc_step.sem, 1)
                        dve.wait_ge(bc_step.sem, bc_step.at(p, 3))
                        dve.tensor_tensor(bc_rest, bc_rest, bc_parts[:, 1, :], ALU.subtract).then_inc(bc_step.sem, 1)
                        dve.wait_ge(bc_step.sem, bc_step.at(p, 4))
                        dve.tensor_copy(bc_parts[:, 2, :], bc_rest).then_inc(bc_ready.sem, 1)
                    if i == 12:
                        dve.wait_ge(pre_ready.sem, pre_ready.at(p, KI))
                        dve.scalar_tensor_tensor(expo, pre, -1.0, pre, ALU.mult, ALU.min).then_inc(abs_ready.sem, 1)
                    if i == 14:
                        dve.wait_ge(exp_ready.sem, exp_ready.at(p, 1))
                        dve.tensor_scalar(u[:, d], expo, 1.0, None, ALU.add).then_inc(one_ready.sem, 1)
                    if i == 15:
                        dve.wait_ge(one_ready.sem, one_ready.at(p, 1))
                        dve.scalar_tensor_tensor(expo, u[:, d], -1.0, expo, ALU.add, ALU.subtract).then_inc(soft_step.sem, 1)
                    if i == 16:
                        dve.wait_ge(soft_step.sem, soft_step.at(p, 1))
                        dve.scalar_tensor_tensor(pre, pre, 0.0, expo, ALU.max, ALU.subtract).then_inc(soft_step.sem, 1)
                    if i == 17:
                        dve.wait_ge(soft_step.sem, soft_step.at(p, 2))
                        dve.wait_ge(log_ready.sem, log_ready.at(p, 1))
                        dve.tensor_tensor(dt[:, d], dt[:, d], pre, ALU.add).then_inc(dt_ready.sem, 1)
                    if i == 18:
                        dve.wait_ge(dt_ready.sem, dt_ready.at(p, 1))
                        dve.wait_ge(in_ready.sem, in_ready.at(p, 1))
                        dve.tensor_tensor(u[:, d], dt[:, d], xsT[:, :, :], ALU.mult).then_inc(u_ready.sem, 1)
                    yield

            def post(b, d):
                for i in range(STEPS["post"]):
                    if i == 4:
                        residual(b, BANK_P, 2 * b + d, gate_l1, GATE_SSM, gate1_in, post_mm, post_part, post_done)
                    yield

            def glu(b):
                for i in range(STEPS["glu"]):
                    if 7 <= i < 7 + KG:
                        m = i - 7
                        dve.wait_ge(glu_silu.sem, glu_silu.at(b, 1))
                        dve.wait_ge(glu_mm.sem, glu_mm.at(b, KG + m + 1))
                        dve.tensor_tensor(hidden[:, KG + m, :], ps[:, BANK_P + m % 2, 0:NB], hidden[:, m, :], ALU.mult).then_inc(glu_ready.sem, 1)
                    if i == STEPS["glu"] - 1:
                        residual(b, BANK_P, b, gate_l1, GATE_GLU, gate1_in, res_mm[RES_GLU], res_part[RES_GLU], res_done[RES_GLU])
                    yield

            def layer0(b):
                yield from norm(b, LN_ATT, None)
                yield from qkv(b)
                yield from heads(b, 0)
                yield from heads(b, 1)
                yield from project(b)
                yield from norm(b, LN_MLP, (res_done[RES_ATT], b))
                yield from idle(STEPS["up"])
                yield from down(b)
                yield from norm(b, LN_SSM, (res_done[RES_MLP], b))

            def close(b):
                yield from norm(b, LN_GLU, (post_done, 2 * b + 1))
                yield from glu(b)

            def times_C(r, i, e, last):
                if e == 0 and last:
                    dve.wait_ge(BC_mm.sem, BC_mm.at(r + AHEAD, 1))
                elif e == 0:
                    dve.wait_ge(B_ready.sem, B_ready.at(r + AHEAD, 1))
                dve.wait_ge(scan_done.sem, scan_done.at(r, e + 1))
                h = hst[:, i % NR, 2 * e:2 * e + 2, :]
                C = ps[:, BANK_BC + i % 2:BANK_BC + i % 2 + 1, NB:2 * NB].to_broadcast([P, 2, NB])
                dve.tensor_tensor(h, h, C, ALU.mult).then_inc(hC_ready.sem, 1)

            def gate_y(p, d):
                dve.wait_ge(y_mm.sem, y_mm.at(p * NS + (NS - 1), 1))
                dve.wait_ge(in_ready.sem, in_ready.at(p, 2))
                dve.tensor_tensor(gT[:, :, :].rearrange("p k n -> p (k n)"), ps[:, BANK_Y:BANK_Y + 2, :].rearrange("p a n -> p (a n)"),
                                  szT[:, d].rearrange("p k n -> p (k n)"), ALU.mult).then_inc(g_ready.sem, 1)

            def state_of(p, d, very_first, very_last, plan):
                way = slice(None) if d == 0 else slice(None, None, -1)

                def state(n, e):
                    r = p * NS + n
                    if n == BEHIND and e == 0 and not very_first:
                        gate_y(p - 1, 1 - d)
                    dve.wait_ge(uB_ready.sem, uB_ready.at(r, e + 1))
                    if e == 0:
                        dve.wait_ge(y_mm.sem, y_mm.at(r, 1 - NR))
                    dve.wait_ge(dA_ready.sem, dA_ready.at(r, e + 1))
                    pair = lambda t: t[:, 2 * e:2 * e + 2, :].rearrange("p k n -> p (k n)")[:, way]
                    dve.tensor_tensor_scan(pair(hst[:, n % NR]), ps[:, plan.bank[2 * n + e], :][:, way],
                                           uB[:, (2 * n + e) % NU].rearrange("p k n -> p (k n)")[:, way],
                                           0.0, ALU.mult, ALU.add).then_inc(scan_done.sem, 1)
                    if not (very_first and n == 0):
                        times_C(r - 1, n + NR - 1, e, very_last and n - 1 + AHEAD >= NS)

                return state

            def period(b, has_prev, has_next):
                l0 = layer0(b + 1) if has_next else None

                def forward():
                    yield from prepare(2 * b + 1, 1)
                    if has_prev:
                        yield from post(b - 1, 1)
                        yield from close(b - 1)
                    if has_next:
                        for i in range(L0_FIRST):
                            next(l0)
                            yield

                def backward():
                    yield from post(b, 0)
                    if has_next:
                        yield from l0
                        yield from prepare(2 * b + 2, 0)

                plan = Plan(0, has_prev, has_next)
                interleave(state_of(2 * b, 0, not has_prev, False, plan), forward(), plan)
                plan = Plan(1, has_prev, has_next)
                interleave(state_of(2 * b + 1, 1, False, not has_next, plan), backward(), plan)

            for _ in layer0(0):
                pass
            for _ in prepare(0, 0):
                pass
            period(0, False, True)
            with dve.Fori(1, NBLK - 1) as b:
                period(b, True, True)
            period(NBLK - 1, True, False)
            for e in range(2):
                times_C(2 * NBLK * NS - 1, NS - 1, e, True)
            gate_y(2 * NBLK - 1, 1)
            for _ in post(NBLK - 1, 1):
                pass
            for _ in close(NBLK - 1):
                pass

        @block.tensor
        def _(pe):
            pe.wait_ge(silu_ready, 1)
            pe.wait_ge(mods_in, N_MODS)
            pe.wait_ge(consts_ready, 5)
            of_kind = [(wada, 1, 0), (wada, 1, 1), (wada, 1, 3), (wada, 1, 4),
                       (wada1[0], 0, 0), (wada1[0], 0, 1), (wada1[1], 0, 0), (wada1[1], 0, 1)]
            conds = (cond_col, silu_col)
            for i, (w, cn, col) in enumerate(of_kind):
                for m in range(KD):
                    o = (i * KD + m) * B
                    for k in range(KD):
                        pe.matmul(ps[:, 0, o:o + B], w[:, k, col * D + m * P:col * D + (m + 1) * P], conds[cn][:, k, :],
                                  start=(k == 0), stop=(k == KD - 1))
            for i, (w, cn, col) in enumerate(((wada, 1, 2), (wada, 1, 5), (wada1[0], 0, 2), (wada1[1], 0, 2))):
                o = ps[0:B, 1 + i // 2, (i % 2) * D:(i % 2 + 1) * D]
                for k in range(KD):
                    pe.matmul(o, conds[cn][:, k, :], w[:, k, col * D:(col + 1) * D], start=(k == 0), stop=False)
                last = pe.matmul(o, ones_row[:, 0:B], gate_bias[:, i, :], start=False, stop=True)
            last.then_inc(mods_mm, 1)
            pe.wait_ge(rows_ready, 1)
            pe.wait_ge(weights_in, N_WEIGHTS)
            pe.wait_ge(mods_ready, 2 * KI)

            def idle(n):
                for i in range(n):
                    yield

            def transpose_block(src):
                for c in range(KD):
                    for j in range(TT):
                        last = pe.transpose(ps[:, BANK_P, c * NB + j * P:c * NB + (j + 1) * P], src[:, j, c * P:(c + 1) * P], ident[:, :])
                return last

            def product(i, lhsT, rhs, ks, kn):
                for k in ks:
                    last = pe.matmul(ps[:, BANK_P + i % 2, 0:NB], lhsT(k), rhs[:, k, :], start=(k == 0), stop=(k == kn - 1))
                return last

            def to_tokens(bank, j, act_T, w, ks, kn, bias=None):
                o = ps[:, bank, j * D:(j + 1) * D]
                if bias is not None and ks[0] == 0:
                    pe.matmul(o, ones_row[:, :], bias, start=True, stop=False)
                for k in ks:
                    last = pe.matmul(o, act_T[:, k, j * P:(j + 1) * P], w[:, k, :], start=(k == 0 and bias is None), stop=(k == kn - 1))
                return last

            def norm(b, s):
                for i in range(STEPS["norm"]):
                    if i == 3:
                        pe.wait_ge(xn_ready[s].sem, xn_ready[s].at(b, 1))
                        transpose_block(xn).then_inc(xnT_mm[s].sem, 1)
                    yield

            def qkv(b):
                for i in range(STEPS["qkv"]):
                    if i == 0:
                        pe.wait_ge(hT_ready[LN_ATT].sem, hT_ready[LN_ATT].at(b, 1))
                    if 2 <= i < 2 + KQ:
                        pe.wait_ge(q_ready.sem, q_ready.at(b, i - 1))
                    elif 2 + KQ <= i < 10:
                        pe.wait_ge(kv_ready.sem, kv_ready.at(b, i - 1 - KQ))
                    if i < 2 * KQ:
                        w, m = (wq, i) if i < KQ else (wk, i - KQ)
                        product(i, lambda k: w[:, k, 4 * m:4 * m + 4, :].rearrange("p h e -> p (h e)"), hT, range(KD), KD).then_inc(qkv_mm.sem, 1)
                    elif i < 2 * KQ + TT:
                        j = i - 2 * KQ
                        for k in range(KD):
                            last = pe.matmul(ps[:, BANK_P + i % 2, 0:D], hT[:, k, j * P:(j + 1) * P], wv[:, k, :], start=(k == 0), stop=(k == KD - 1))
                        last.then_inc(qkv_mm.sem, 1)
                    yield

            def heads(b, ti):
                keys, nk = P * (ti + 1), ti + 1
                for i in range(STEPS["heads"]):
                    if i % 4 == 2 and 1 <= i // 4 < 1 + H // 2:
                        j = i // 4 - 1
                        g = ti * H // 2 + j
                        pe.wait_ge(probsT_ready.sem, probsT_ready.at(b, g + 1))
                        for e in range(2):
                            h = j // 4 * 8 + e * 4 + j % 4
                            for k in range(nk):
                                last = pe.matmul(ps[:, BANK_P + g % 2, e * HD:(e + 1) * HD], probsT[:, (k * 2 + e) * P:(k * 2 + e + 1) * P],
                                                 v[:, k, h * HD:(h + 1) * HD], start=(k == 0), stop=(k == nk - 1))
                        last.then_inc(pv_mm.sem, 1)
                    if i % 4 == 3 and i // 4 < H // 2:
                        g = ti * H // 2 + i // 4
                        pe.wait_ge(probs_ready.sem, probs_ready.at(b, 2 * (g + 1)))
                        for k in range(nk):
                            for e in range(2):
                                o = (k * 2 + e) * P
                                last = pe.transpose(ps[:, BANK_P + g % 2, o:o + P], probs[:, e, k * P:(k + 1) * P], ident[:, :])
                        last.then_inc(probsT_mm.sem, 1)
                    if i % 4 == 0 and i // 4 < H // 2:
                        j = i // 4
                        g = ti * H // 2 + j
                        if g == 0:
                            pe.wait_ge(q_ready.sem, q_ready.at(b, KQ))
                            pe.wait_ge(kv_ready.sem, kv_ready.at(b, KQ + TT))
                        if g >= 2:
                            pe.wait_ge(o_raw.sem, o_raw.at(b, g - 1))
                        rows = slice(HP * (j % 4), HP * (j % 4 + 1))
                        for e in range(2):
                            c = j // 4 * 2 + e
                            pe.matmul(ps[:, BANK_P + g % 2, e * T:e * T + keys], qT[rows, c, ti * P:(ti + 1) * P], kT[rows, c, 0:keys],
                                      start=True, stop=False)
                            last = pe.matmul(ps[:, BANK_P + g % 2, e * T + ti * P:e * T + (ti + 1) * P], ident_b[:, :], causal_b[:, :],
                                             start=False, stop=True)
                        last.then_inc(score_mm.sem, 1)
                    yield

            def project(b):
                for i in range(STEPS["proj"]):
                    if i == 0:
                        pe.wait_ge(o_ready.sem, o_ready.at(b, TT))
                        transpose_block(o_sb).then_inc(oT_mm.sem, 1)
                    if i in (1, 2):
                        pe.wait_ge(oT_ready.sem, oT_ready.at(b, 1))
                        last = to_tokens(BANK_P + 1, i - 1, oT, wproj, range(KD), KD, bias_rows[:, 0, :])
                        if i == 2:
                            last.then_inc(res_mm[RES_ATT].sem, 1)
                    yield

            def up(b):
                for i in range(STEPS["up"]):
                    if i == 0:
                        pe.wait_ge(hT_ready[LN_MLP].sem, hT_ready[LN_MLP].at(b, 1))
                    if i < KF:
                        if i >= 2:
                            pe.wait_ge(up_ready.sem, up_ready.at(b, i - 1))
                        product(i, lambda k: w1[:, k, i * P:(i + 1) * P], hT, range(KD), KD).then_inc(up_mm.sem, 1)
                    yield

            def down(b):
                for i in range(STEPS["down"]):
                    if i == 0:
                        pe.wait_ge(gelu_ready.sem, gelu_ready.at(b, 1))
                    if i < 8:
                        last = to_tokens(BANK_P, i // 4, hidden, w2, range(i % 4 * 2, i % 4 * 2 + 2), KF, bias_rows[:, 1, :])
                        if i == 7:
                            last.then_inc(res_mm[RES_MLP].sem, 1)
                    yield

            def prepare(p, d, b):
                for i in range(STEPS["ins"]):
                    if i == 0:
                        pe.wait_ge(hT_ready[LN_SSM].sem, hT_ready[LN_SSM].at(b, 1))
                    if i < 2 * KI:
                        if i >= 2:
                            pe.wait_ge(in_raw.sem, in_raw.at(p, i - 1))
                        product(i, lambda k: w_in[d][:, k, i * P:(i + 1) * P], hT_ssm, range(KD), KD).then_inc(in_mm.sem, 1)
                    yield
                for i in range(STEPS["dts"]):
                    if i == 0:
                        pe.wait_ge(in_ready.sem, in_ready.at(p, 1))
                    if i < 2 + 2 * KI:
                        m = i // 2 - 1 if i >= 2 else KI
                        bank = i // 2 % 2
                        if i in (4, 5):
                            pe.wait_ge(bc_step.sem, bc_step.at(p, 2))
                        if i >= 6 and i % 2 == 0:
                            pe.wait_ge(pre_ready.sem, pre_ready.at(p, m - 1))
                        last = product(bank, lambda k: w_xp[d][:, k, m * P:(m + 1) * P], xsT, range(i % 2 * 2, i % 2 * 2 + 2), KI)
                        if i == 1:
                            last.then_inc(bc_mm.sem, 1)
                        elif i % 2 == 1:
                            last.then_inc(dt_mm.sem, 1)
                    yield

            def post(b, d):
                for i in range(STEPS["post"]):
                    if i == 0:
                        pe.wait_ge(g_ready.sem, g_ready.at(2 * b + d, 1))
                    if i < 4:
                        last = to_tokens(BANK_P, i // 2, gT, w_out[d], range(i % 2 * 2, i % 2 * 2 + 2), KI)
                        if i == 3:
                            last.then_inc(post_mm.sem, 1)
                    if i == 5:
                        pe.wait_ge(post_part.sem, post_part.at(2 * b + d, 1))
                    yield

            def glu(b):
                for i in range(STEPS["glu"]):
                    if i == 0:
                        pe.wait_ge(hT_ready[LN_GLU].sem, hT_ready[LN_GLU].at(b, 1))
                    if i < KG:
                        if i >= 2:
                            pe.wait_ge(glu_raw.sem, glu_raw.at(b, i - 1))
                        product(i, lambda k: wg1[:, k, i * P:(i + 1) * P], hT, range(KD), KD).then_inc(glu_mm.sem, 1)
                    if 6 <= i < 6 + KG:
                        m = i - 6
                        if m < 2:
                            pe.wait_ge(glu_raw.sem, glu_raw.at(b, KG - 1 + m))
                        else:
                            pe.wait_ge(glu_ready.sem, glu_ready.at(b, m - 1))
                        product(m, lambda k: wg2[:, k, m * P:(m + 1) * P], hT, range(KD), KD).then_inc(glu_mm.sem, 1)
                    if 11 <= i < 15:
                        if i == 11:
                            pe.wait_ge(glu_ready.sem, glu_ready.at(b, KG))
                        last = to_tokens(BANK_P, (i - 11) // 2, hidden[:, KG:2 * KG, :], wg3, range((i - 11) % 2 * 2, (i - 11) % 2 * 2 + 2), KG)
                        if i == 14:
                            last.then_inc(res_mm[RES_GLU].sem, 1)
                    yield

            def layer0(b):
                yield from norm(b, LN_ATT)
                yield from qkv(b)
                yield from heads(b, 0)
                yield from heads(b, 1)
                yield from project(b)
                yield from norm(b, LN_MLP)
                yield from up(b)
                yield from down(b)
                yield from norm(b, LN_SSM)

            def close(b):
                yield from norm(b, LN_GLU)
                yield from glu(b)

            def spread(bank, side, d, group, n):
                return pe.matmul(ps[:, bank, side * NB:(side + 1) * NB], pick[0:PARTS * HP, n % HP:n % HP + 1].to_broadcast([PARTS * HP, P]),
                                 bc_rows[:, d, group + n // HP, :], start=True, stop=True)

            def spread_B(p, d, n):
                r = p * NS + n
                if n == 0:
                    pe.wait_ge(bc_in.sem, bc_in.at(p, bc_in.per))
                pe.wait_ge(B_ready.sem, B_ready.at(r, -1))
                return spread(BANK_BC + (n + 1) % 2, 0, d, 0, n)

            def spread_BC(p, d, n, last):
                pe.wait_ge(hC_ready.sem, hC_ready.at(p * NS + n, 2 - 2 * 2))
                if n + AHEAD < NS:
                    spread_B(p, d, n + AHEAD)
                elif not last:
                    spread_B(p + 1, 1 - d, n + AHEAD - NS)
                spread(BANK_BC + n % 2, 1, d, 2, n).then_inc(BC_mm.sem, 1)

            def start_y(p, d):
                pe.wait_ge(g_ready.sem, g_ready.at(p, 0))
                for c in range(KI):
                    pe.matmul(ps[:, BANK_Y + c // 2, c % 2 * NB:(c % 2 + 1) * NB], skip_diag[:, d, c, :], xsT[:, c, :],
                              start=(c % 2 == 0), stop=False, skip_group_check=True)

            def sum_state(r, n, e):
                pe.wait_ge(hC_ready.sem, hC_ready.at(r, e + 1))
                last = pe.matmul(ps[:, BANK_Y + e, :], ident[:, :], hst[:, n % NR, 2 * e:2 * e + 2, :].rearrange("p k n -> p (k n)"),
                                 start=False, stop=(n == NS - 1), skip_group_check=True)
                if e == 1:
                    last.then_inc(y_mm.sem, 1)

            def state_of(p, d, very_first, very_last):
                def state(n, e):
                    if e == 0:
                        spread_BC(p, d, n, very_last)
                        if n == BEHIND:
                            start_y(p, d)
                    if n >= BEHIND:
                        sum_state(p * NS + n - BEHIND, n - BEHIND, e)
                    elif not very_first:
                        sum_state(p * NS + n - BEHIND, NS + n - BEHIND, e)

                return state

            def period(b, has_prev, has_next):
                l0 = layer0(b + 1) if has_next else None

                def forward():
                    yield from prepare(2 * b + 1, 1, b)
                    if has_prev:
                        yield from post(b - 1, 1)
                        yield from close(b - 1)
                    if has_next:
                        for i in range(L0_FIRST):
                            next(l0)
                            yield

                def backward():
                    yield from post(b, 0)
                    if has_next:
                        yield from l0
                        yield from prepare(2 * b + 2, 0, b + 1)

                def free(p, plan):
                    def before(j):
                        if j in plan.scanned:
                            n, e = plan.scanned[j] // 2, plan.scanned[j] % 2
                            pe.wait_ge(scan_done.sem, scan_done.at(p * NS + n, e + 1))

                    return before

                plan = Plan(0, has_prev, has_next)
                interleave(state_of(2 * b, 0, not has_prev, False), forward(), plan, free(2 * b, plan))
                plan = Plan(1, has_prev, has_next)
                interleave(state_of(2 * b + 1, 1, False, not has_next), backward(), plan, free(2 * b + 1, plan))

            for _ in layer0(0):
                pass
            for _ in prepare(0, 0, 0):
                pass
            for n in range(AHEAD):
                spread_B(0, 0, n).then_inc(BC_mm.sem, 1)
            period(0, False, True)
            with pe.Fori(1, NBLK - 1) as b:
                period(b, True, True)
            period(NBLK - 1, True, False)
            for n in range(NS - BEHIND, NS):
                for e in range(2):
                    sum_state((2 * NBLK - 1) * NS + n, n, e)
            for _ in post(NBLK - 1, 1):
                pass
            for _ in close(NBLK - 1):
                pass


_MATRICES = ['L0_cond_Wqkv', 'L0_cond_Wproj', 'L0_cond_W1', 'L0_cond_W2', 'L0_cond_Wada', 'L1_cond_adaln_mamba_w',
             'L1_cond_adaln_mlp_w', 'L1_cond_mlp_w1', 'L1_cond_mlp_w2', 'L1_cond_mlp_w3',
             'L1_cond_fwd_in_w', 'L1_cond_fwd_xproj_w', 'L1_cond_fwd_out_w',
             'L1_cond_bwd_in_w', 'L1_cond_bwd_xproj_w', 'L1_cond_bwd_out_w']


def kernel(**inputs):
    import numpy as _np
    import concourse.bacc as _bacc
    from concourse import mybir as _mybir
    from concourse.bass_utils import run_bass_kernel_spmd as _run

    get = lambda name: _np.asarray(inputs[name])
    P, D = 128, 256
    third = lambda name, i: get(name)[i * D:(i + 1) * D]
    by_channel = lambda a: a.reshape(-1, P).T
    l0, l1, mamba, glu = 'L0_cond_', 'L1_cond_', 'L1_cond_adaln_mamba_b', 'L1_cond_adaln_mlp_b'
    shifts = [third(l0 + 'bada', i) for i in (0, 1, 3, 4)] + [third(mamba, 0), third(mamba, 1), third(glu, 0), third(glu, 1)]
    cond = get('cond_1024')
    columns = _np.concatenate(
        [cond[:, k * P:(k + 1) * P].T for k in range(D // P)] + [by_channel(a) for a in shifts + [
            get(l0 + 'g1'), get(l0 + 'g2'), get(l0 + 'be1'), get(l0 + 'be2'), get(l0 + 'b1'),
            get(l1 + 'fwd_dt_bias'), get(l1 + 'bwd_dt_bias'), get(l1 + 'fwd_D'), get(l1 + 'bwd_D')]], axis=1)
    rows = _np.concatenate([third(l0 + 'bada', 2), third(l0 + 'bada', 5), third(mamba, 2), third(glu, 2),
                            get(l0 + 'bproj'), get(l0 + 'b2')])[None, :]
    A_log = _np.concatenate([get(l1 + n + 'A_log')[k * P:(k + 1) * P] for n in ('fwd_', 'bwd_') for k in range(4)], axis=1)

    nc = _bacc.Bacc("TRN2", target_bir_lowering=False, num_devices=1)
    arrays, args = {}, []
    for name, a in [('x', get('x')), ('columns', columns), ('rows', rows), ('A_log', A_log)] + [(n, get(n)) for n in _MATRICES]:
        a = _np.ascontiguousarray(a)
        arrays[f"in_{name}_dram"] = a
        args.append(nc.dram_tensor(f"in_{name}_dram", a.shape, _mybir.dt.from_np(a.dtype), kind="ExternalInput").ap())
    args.append(nc.dram_tensor("out_0_dram", get('x').shape, _mybir.dt.float32, kind="ExternalOutput").ap())
    args.append(nc.dram_tensor("gate_rows_dram", (cond.shape[0], 4 * D), _mybir.dt.float32, kind="Internal").ap())
    cond_transformer_mamba_kernel(nc, *args)
    r = _run(nc, [arrays], core_ids=[0])
    return r.results[0]["out_0_dram"]
```

```python
import math
import numpy as np
import concourse.bass as bass
from concourse import mybir
from contextlib import ExitStack


class Flow:

    def __init__(self, sem, per, start=0):
        self.sem, self.per, self.start = sem, per, start

    def at(self, rnd, k):
        return rnd * self.per + (self.start + k)


def cond_transformer_mamba_kernel(
    nc, x, columns, rows, A_log, Wqkv, Wproj, W1, W2, Wada, wmamba, wglu, glu_w1, glu_w2, glu_w3,
    f_in, f_xproj, f_out, b_in, b_xproj, b_out, out, gate_rows,
):
    f32, bf16 = mybir.dt.float32, mybir.dt.bfloat16
    ALU, ACT, AX = mybir.AluOpType, mybir.ActivationFunctionType, mybir.AxisListType

    P = 128
    B, T, D = x.shape
    H = 16
    HD = D // H
    HP = 32
    KD = D // P
    NB = T
    NBLK = B
    TT = NB // P
    KF = W1.shape[1] // P
    DI = f_out.shape[0]
    KI = DI // P
    NS = A_log.shape[1] // (2 * KI)
    KG = glu_w1.shape[1] // P
    KQ = H * HP // P
    EPS = 1e-5
    NEG = -1e30
    NR = 4
    AHEAD = 3
    BEHIND = 2
    NU = 4
    PARTS = 3
    LN_ATT, LN_MLP, LN_SSM, LN_GLU = range(4)
    RES_ATT, RES_MLP, RES_GLU = range(3)
    GATE_SSM, GATE_GLU = 0, 1

    PARITY = 1
    LIGHT, HEAVY, LONG, AMONG = 1.0, 2.0, 2.0, 1.0
    STEPS = dict(norm=6, qkv=11, heads=37, proj=5, up=12, down=10, ins=12, dts=19, post=7, glu=17)
    ROOM = dict(norm=[HEAVY, LIGHT, HEAVY, HEAVY, LIGHT, LIGHT], qkv=[HEAVY] * 10 + [LIGHT], heads=[LIGHT] * STEPS["heads"],
                proj=[LIGHT, HEAVY, HEAVY, LIGHT, HEAVY], up=[HEAVY] * 8 + [LIGHT, LIGHT, LONG, LIGHT], down=[HEAVY] * 8 + [LIGHT, HEAVY],
                ins=[HEAVY] * 8 + [LIGHT, LIGHT, LONG, LIGHT], dts=[HEAVY] * 10 + [LIGHT] * 2 + [HEAVY] * 3 + [LONG] + [HEAVY] * 3,
                post=[HEAVY] * 4 + [LIGHT, HEAVY, LIGHT], glu=[HEAVY] * 4 + [LIGHT, LONG] + [HEAVY] * 4 + [LIGHT] + [HEAVY] * 4 + [LIGHT, HEAVY])
    FIRST_HALF, LAST_HALF = 4, 124

    LONG_STEPS = [{("first", "norm", 2), ("last", "glu", 5)}, {("first", "norm", 2), ("first", "up", 10), ("first", "ins", 10)}]
    NO_PRODUCT = {(s, k) for s, ks in dict(norm=(0, 1, 2, 3), up=(10, 11), ins=(10, 11), dts=range(10, 19), glu=(5,)).items() for k in ks}
    L0_FIRST = STEPS["norm"] + STEPS["qkv"] + STEPS["heads"]
    BANK_A, BANK_BC, BANK_Y, BANK_P = 0, 2, 4, 6

    def stage(chain, name, *part):
        return [(chain, name, k) for k in range(*(part or (STEPS[name],)))]

    def meanwhile(mine, others):
        steps, done = [], 0
        for k, step in enumerate(mine):
            steps.append(step)
            upto = len(others) * (k + 1) // len(mine)
            steps += others[done:upto]
            done = upto
        return steps

    def order(d, has_prev, has_next):
        if d == 0:
            first = has_next * (stage("first", "norm") + stage("first", "qkv") + stage("first", "heads"))
            if not has_prev:
                return stage("own", "ins") + stage("own", "dts") + first
            return (stage("own", "ins", 0, 10) + meanwhile(stage("last", "post"), stage("own", "ins", 10, 12))
                    + stage("own", "dts", 0, 2) + meanwhile(stage("own", "dts", 2, 12), stage("last", "norm", 0, 4))
                    + meanwhile(stage("own", "dts", 12, 19), stage("last", "norm", 4, 6) + stage("last", "glu", 0, 5))
                    + stage("last", "glu", 5, STEPS["glu"]) + first)
        if not has_next:
            return stage("last", "post")
        rest = sum([stage("first", name) for name in ("proj", "norm", "up", "down", "norm", "ins")], stage("first", "heads"))
        return rest + stage("first", "dts", 0, 12) + meanwhile(stage("first", "dts", 12, 19), stage("last", "post"))

    class Plan:

        def __init__(self, d, has_prev, has_next):
            self.steps = order(d, has_prev, has_next)
            rooms = [self.room(j) for j in range(len(self.steps))]
            self.behind = [[] for i in range(2 * NS)]
            self.ahead = {}
            self.scanned = {}
            self.bank = [BANK_A + i % 2 for i in range(2 * NS)]
            pending = None
            start = FIRST_HALF if d == 0 or not has_next else 0
            rest = sum(r for r, step in zip(rooms, self.steps) if step[1] != "heads")
            heads = sum(step[1] == "heads" for step in self.steps) + 1
            at, scale = float(start), (LAST_HALF - start - heads) / rest
            for j, step in enumerate(self.steps):
                if step[1] == "heads":
                    if step[2] == 0 and math.ceil(at) % 2 != PARITY:
                        at += 1
                    i = math.ceil(at)
                    at = i + 1
                else:
                    i = int(at)
                    at += rooms[j] * scale
                self.behind[i].append(j)
                if pending is not None and step[1:] not in NO_PRODUCT:
                    self.scanned[j], pending = pending, None
                if step in LONG_STEPS[d] and self.bank[i + 1] < BANK_P:
                    self.ahead[j] = [i + 1, i + 2]
                    self.bank[i + 1], self.bank[i + 2] = BANK_P, BANK_P + 1
                    pending = i + 2
            self.before = [max([k for k in range(i) if self.bank[k] == self.bank[i]], default=i - 2 if self.bank[i] < BANK_P else None)
                           for i in range(2 * NS)]

        def room(self, j):
            chain, name, k = self.steps[j]
            if 0 < j and self.steps[j - 1][0] != chain and j + 1 < len(self.steps) and self.steps[j + 1][0] != chain:
                return AMONG
            return ROOM[name][k]

    def interleave(state, chains, plan, before=None):
        for i in range(2 * NS):
            state(i // 2, i % 2)
            for j in plan.behind[i]:
                if before:
                    before(j)
                next(chains[plan.steps[j][0]])

    x_tiles = x.rearrange("b (h p) d -> p (b h) d", p=P)
    out_tiles = out.rearrange("b (h p) d -> p (b h) d", p=P)

    ctx = ExitStack()
    with ctx:
        def sb(name, shape, dt=f32):
            return ctx.enter_context(nc.sbuf_tensor(name, shape, dt))

        def sem(name):
            return ctx.enter_context(nc.semaphore(name))

        def flow(name, per=1, start=0):
            return Flow(sem(name), per, start)

        wq = sb("wq", [P, KD, H, HP])
        wk = sb("wk", [P, KD, H, HP])
        wv = sb("wv", [P, KD, D])
        wproj = sb("wproj", [P, KD, D])
        w1 = sb("w1", [P, KD, KF * P])
        w2 = sb("w2", [P, KF, D])
        w_in = [sb(f"w_in{d}", [P, KD, 2 * DI]) for d in range(2)]
        w_xp = [sb(f"w_xp{d}", [P, KI, DI + 2 * NS]) for d in range(2)]
        w_out = [sb(f"w_out{d}", [P, KI, D]) for d in range(2)]
        wg1 = sb("wg1", [P, KD, KG * P])
        wg2 = sb("wg2", [P, KD, KG * P])
        wg3 = sb("wg3", [P, KG, D])
        bias_rows = sb("bias_rows", [1, 2, D])
        col_in = sb("col_in", [P, columns.shape[1]])
        cols = [0]

        def column(*shape):
            at, n = cols[0], int(np.prod(shape))
            cols[0] += n
            part = col_in[:, at:at + n]
            return part if len(shape) == 1 else part.rearrange("p (a b) -> p a b", b=shape[1])

        cond_col = column(KD, B)
        mod_bias = column(8, KD)
        ln_g, ln_b = column(2, KD), column(2, KD)
        b1_col = column(KF)
        dtb_col, D_col = column(2, KI), column(2, KI)
        A = sb("A", [P, 2, KI, NS])
        ident = sb("ident", [P, P])
        ident_b = sb("ident_b", [P, P], bf16)
        causal_b = sb("causal_b", [P, P], bf16)
        pick = sb("pick", [P, HP], bf16)
        ones_row = sb("ones_row", [1, P])
        zeros = sb("zeros", [P, 2])
        skip_diag = sb("skip_diag", [P, 2, KI, P])
        silu_col = sb("silu_col", [P, KD, B])
        mods = sb("mods", [P, 8, KD, B])
        mod_scale = sb("mod_scale", [P, 4, KD, B])
        mod_shift = sb("mod_shift", [P, 4, KD, B])
        gate_l0 = sb("gate_l0", [P, 2, D])
        gate_l1 = sb("gate_l1", [P, 2, D])
        xs_all = sb("xs_all", [P, NBLK * TT, D])
        xn = sb("xn", [P, TT, D])
        hT = sb("hT", [P, KD, NB])
        hT_ssm = sb("hT_ssm", [P, KD, NB])
        stats = sb("stats", [P, TT, 6])
        mv = sb("mv", [P, TT, 2])
        rstd = sb("rstd", [P, TT])
        qk = sb("qk", [P, 2 * KQ, NB])
        qT, kT = qk[:, 0:KQ, :], qk[:, KQ:2 * KQ, :]
        v = sb("v", [P, TT, D])
        probs = sb("probs", [P, 2, T])
        probsT = sb("probsT", [P, TT * 2 * P])
        o_sb = sb("o_sb", [P, TT, D])
        prime = sb("prime", [P, 6])
        nmax = sb("nmax", [P, 2])
        psum_exp = sb("psum_exp", [P, TT, H])
        rsum = sb("rsum", [P, TT, H])
        xsT = sb("xsT", [P, KI, NB])
        szT = sb("szT", [P, 2, KI, NB])
        dt = sb("dt", [P, 2, KI, NB])
        u = sb("u", [P, 2, KI, NB])
        bc_parts = sb("bc_parts", [P, PARTS, NB], bf16)
        bc_rows = sb("bc_rows", [PARTS * HP, 2, 4, NB], bf16)
        gT = sb("gT", [P, KI, NB])
        B_sb = sb("B_sb", [P, NR, NB])
        uB = sb("uB", [P, NU, 2, NB])
        hst = sb("hst", [P, NR, KI, NB])

        part = xn
        bc_rest = probs[:, 0, :]
        oT = v
        hidden = qk
        pre, expo = qT, kT
        flat = lambda t, n: t.rearrange("p a b -> p (a b)")[:, 0:KD * n].rearrange("p (k n) -> p k n", k=KD)
        wada = flat(hst[:, :, :, :].rearrange("p r k n -> p r (k n)"), 6 * D)
        wada1 = [flat(uB[:, :, :, :].rearrange("p r k n -> p r (k n)"), 3 * D), flat(qk[:, :, :], 3 * D)]
        mod_rows = gT[0:B, :, :].rearrange("p a b -> p (a b)")
        gate_bias = B_sb[0:1, :, :]

        ps = ctx.enter_context(nc.psum_tensor("ps", [P, 8, 2 * NB], f32))

        mods_in, x_in, weights_in, rows_out, out_done = map(sem, ("mods_in", "x_in", "weights_in", "rows_out", "out_done"))
        pads_zero, pool_step, consts_ready, silu_ready, A_ready, mods_mm = map(
            sem, ("pads_zero", "pool_step", "consts_ready", "silu_ready", "A_ready", "mods_mm"))
        dve_setup, rows_ready, mods_ready, bn_turns = map(sem, ("dve_setup", "rows_ready", "mods_ready", "bn_turns"))
        gate0_in, gate1_in = flow("gate0_in", 16), flow("gate1_in", 16)
        norm_step = [flow(f"norm_step{s}", 3) for s in range(4)]
        stat_ready = [flow(f"stat_ready{s}") for s in range(4)]
        std_ready = [flow(f"std_ready{s}") for s in range(4)]
        xn_ready = [flow(f"xn_ready{s}") for s in range(4)]
        xnT_mm = [flow(f"xnT_mm{s}") for s in range(4)]
        hT_ready = [flow(f"hT_ready{s}") for s in range(4)]
        qkv_mm, q_ready, kv_ready = flow("qkv_mm", 10), flow("q_ready", 4), flow("kv_ready", 6)
        NG = TT * H // 2
        score_mm, max_ready, probs_ready = flow("score_mm", NG), flow("max_ready", NG), flow("probs_ready", 2 * NG)
        probsT_mm, probsT_ready, pv_mm, o_raw = flow("probsT_mm", NG), flow("probsT_ready", NG), flow("pv_mm", NG), flow("o_raw", NG)
        rsum_ready, o_ready, oT_mm, oT_ready = flow("rsum_ready", TT), flow("o_ready", TT), flow("oT_mm"), flow("oT_ready")
        up_mm, up_ready, gelu_ready = flow("up_mm", KF), flow("up_ready", KF), flow("gelu_ready")
        glu_mm, glu_raw, glu_silu, glu_ready = flow("glu_mm", 2 * KG), flow("glu_raw", KG), flow("glu_silu"), flow("glu_ready", KG)
        res_mm, res_part, res_done = ([flow(f"{n}{r}") for r in range(3)] for n in ("res_mm", "res_part", "res_done"))
        post_mm, post_part, post_done = flow("post_mm"), flow("post_part"), flow("post_done")
        in_mm, in_raw, in_ready = flow("in_mm", 2 * KI), flow("in_raw", 2 * KI), flow("in_ready", 2)
        bc_mm, bc_step, bc_ready, bc_in = flow("bc_mm"), flow("bc_step", 4), flow("bc_ready"), flow("bc_in", 16 * PARTS * 4)
        dt_mm, pre_ready, abs_ready, exp_ready, one_ready, log_ready = (
            flow("dt_mm", KI), flow("pre_ready", KI), flow("abs_ready"), flow("exp_ready"), flow("one_ready"), flow("log_ready"))
        soft_step, dt_ready, u_ready, g_ready = flow("soft_step", 2), flow("dt_ready"), flow("u_ready"), flow("g_ready", 1, 1)
        BC_mm, B_ready = flow("BC_mm"), flow("B_ready", 1, 2)
        dA_ready, uB_ready = flow("dA_ready", 2), flow("uB_ready", 2, 2 * NR)
        scan_done, hC_ready, y_mm = flow("scan_done", 2, 4), flow("hC_ready", 2, 2 * NR), flow("y_mm", 1, NR)

        block = ctx.enter_context(nc.Block())

        @block.sync
        def _(sp):
            sp.dma_start(col_in[:, :], columns).then_inc(mods_in, 16)
            sp.dma_start(gate_bias, rows[:, 0:4 * D].rearrange("a (i n) -> a i n", n=D)).then_inc(mods_in, 16)
            sp.dma_start(wada, Wada.rearrange("(k p) n -> p k n", p=P)).then_inc(mods_in, 16)
            sp.dma_start(wada1[0], wmamba.rearrange("(k p) n -> p k n", p=P)).then_inc(mods_in, 16)
            sp.dma_start(wada1[1], wglu.rearrange("(k p) n -> p k n", p=P)).then_inc(mods_in, 16)
            sp.dma_start(xs_all[:, :, :], x_tiles).then_inc(x_in, 16)
            sp.wait_ge(pads_zero, 2)
            for w, c in ((wq, 0), (wk, 1)):
                for k in range(KD):
                    sp.dma_start(w[:, k, :, 0:HD], Wqkv[k * P:(k + 1) * P, c * D:(c + 1) * D]
                                 .rearrange("p (h e) -> p h e", e=HD)).then_inc(weights_in, 16)
            sp.dma_start(wv[:, :, :], Wqkv[:, 2 * D:3 * D].rearrange("(k p) n -> p k n", p=P)).then_inc(weights_in, 16)
            loads = [(wproj, Wproj), (w1, W1), (w2, W2), (w_in[0], f_in), (w_in[1], b_in), (w_xp[0], f_xproj),
                     (w_xp[1], b_xproj), (w_out[0], f_out), (w_out[1], b_out), (wg1, glu_w1), (wg2, glu_w2), (wg3, glu_w3)]
            for w, src in loads:
                sp.dma_start(w[:, :, :], src.rearrange("(k p) n -> p k n", p=P)).then_inc(weights_in, 16)
            sp.dma_start(A[:, :, :, :].rearrange("p d k n -> p (d k n)"), A_log).then_inc(weights_in, 16)
            sp.dma_start(bias_rows[:, :, :].rearrange("a i n -> a (i n)"), rows[:, 4 * D:6 * D]).then_inc(weights_in, 16)
            sp.wait_ge(rows_ready, 1)
            sp.dma_start(gate_rows, mod_rows).then_inc(rows_out, 16)
            sp.wait_ge(rows_out, 16)

            def load_gates(gates, o, b, half):
                sp.dma_start(gates[:, :, :].rearrange("p g d -> p (g d)"),
                             gate_rows[bass.ds(b, 1), half * 2 * D:(half + 1) * 2 * D].rearrange("a n -> (a n)")
                             .partition_broadcast(P)).then_inc(o.sem, 16)

            def stack_rows(p, d):
                sp.wait_ge(bc_ready.sem, bc_ready.at(p, 1))
                for q in range(4):
                    for k in range(PARTS):
                        sp.dma_start(bc_rows[k * HP:(k + 1) * HP, d, q, :], bc_parts[q * HP:(q + 1) * HP, k, :]).then_inc(bc_in.sem, 16)

            def store(b):
                sp.wait_ge(res_done[RES_GLU].sem, res_done[RES_GLU].at(b, 1))
                sp.dma_start(out_tiles[:, bass.ds(b * TT, TT), :], xs_all[:, bass.ds(b * TT, TT), :]).then_inc(out_done, 16)

            def period(b, has_prev, has_next):
                if has_next:
                    sp.wait_ge(res_done[RES_MLP].sem, res_done[RES_MLP].at(b, 1))
                    load_gates(gate_l0, gate0_in, b + 1, 0)
                stack_rows(2 * b + 1, 1)
                if has_prev:
                    store(b - 1)
                    load_gates(gate_l1, gate1_in, b, 1)
                if has_next:
                    stack_rows(2 * b + 2, 0)

            load_gates(gate_l0, gate0_in, 0, 0)
            load_gates(gate_l1, gate1_in, 0, 1)
            stack_rows(0, 0)
            period(0, False, True)
            with sp.Fori(1, NBLK - 1) as b:
                period(b, True, True)
            period(NBLK - 1, True, False)
            store(NBLK - 1)
            sp.wait_ge(out_done, 16 * NBLK)

        N_MODS, N_WEIGHTS = 16 * 5, 16 * (5 + 12 + 2)

        @block.gpsimd
        def _(pool):
            pool.memset(wq[:, :, :, :], 0.0).then_inc(pads_zero, 1)
            pool.memset(wk[:, :, :, :], 0.0).then_inc(pads_zero, 1)
            pool.memset(ident[:, :], 0.0).then_inc(pool_step, 1)
            pool.memset(causal_b[:, :], 0.0).then_inc(pool_step, 1)
            pool.memset(pick[:, :], 0.0).then_inc(pool_step, 1)
            pool.wait_ge(pool_step, 3)
            pool.affine_select(out=ident[:, :], in_=ident[:, :], compare_op=ALU.not_equal, fill=1.0, base=0,
                               pattern=[[-1, P]], channel_multiplier=1).then_inc(consts_ready, 1)
            pool.affine_select(out=causal_b[:, :], in_=causal_b[:, :], compare_op=ALU.is_ge, fill=NEG, base=0,
                               pattern=[[-1, P]], channel_multiplier=1).then_inc(consts_ready, 1)
            for k in range(PARTS):
                pool.affine_select(out=pick[:, :], in_=pick[:, :], compare_op=ALU.not_equal, fill=1.0, base=-k * HP,
                                   pattern=[[-1, HP]], channel_multiplier=1).then_inc(pool_step, 1)
                pool.wait_ge(pool_step, 4 + k)
            pool.memset(ones_row[:, :], 1.0).then_inc(consts_ready, 1)
            pool.memset(zeros[:, :], 0.0).then_inc(consts_ready, 1)
            pool.wait_ge(consts_ready, 4)
            pool.tensor_copy(ident_b[:, :], ident[:, :]).then_inc(consts_ready, 1)

            def products(p, d, n, i):
                r = p * NS + n
                pool.wait_ge(B_ready.sem, B_ready.at(r, 1))
                for e in range(2):
                    pool.wait_ge(scan_done.sem, scan_done.at(r, e + 1 - NU))
                    pool.tensor_tensor(uB[:, (2 * i + e) % NU], u[:, d, 2 * e:2 * e + 2, :],
                                       B_sb[:, i:i + 1, :].to_broadcast([P, 2, NB]), ALU.mult).then_inc(uB_ready.sem, 1)

            with pool.Fori(0, NBLK) as b:
                for d in range(2):
                    p = b * 2 + d
                    pool.wait_ge(u_ready.sem, u_ready.at(p, 1))
                    for i in range(NR):
                        products(p, d, i, i)
                    with pool.Fori(NR, NS, NR) as n0:
                        for i in range(NR):
                            products(p, d, n0 + i, i)

        @block.scalar
        def _(act):
            act.wait_ge(mods_in, N_MODS)
            act.activation(silu_col[:, :, :], cond_col, ACT.Silu).then_inc(silu_ready, 1)
            act.wait_ge(weights_in, N_WEIGHTS)
            act.activation(A[:, :, :, :], A[:, :, :, :], ACT.Exp).then_inc(A_ready, 1)
            act.activation(prime[:, 0:1], col_in[:, 0:1], ACT.Copy).then_inc(B_ready.sem, B_ready.start)
            act.wait_ge(A_ready, 2)
            act.wait_ge(mods_ready, 1)
            act.wait_ge(consts_ready, 5)

            def norm(b, s, dst):
                for i in range(STEPS["norm"]):
                    if i == 2:
                        act.wait_ge(stat_ready[s].sem, stat_ready[s].at(b, 1))
                        act.activation(rstd[:, :], mv[:, :, 1], ACT.Sqrt).then_inc(std_ready[s].sem, 1)
                    if i == 5:
                        act.wait_ge(xnT_mm[s].sem, xnT_mm[s].at(b, 1))
                        for c in range(KD):
                            col = bass.ds(b, 1)
                            last = act.activation(dst[:, c, :], ps[:, BANK_P, c * NB:(c + 1) * NB], ACT.Identity,
                                                  bias=mod_shift[:, s, c, col], scale=mod_scale[:, s, c, col])
                        last.then_inc(hT_ready[s].sem, 1)
                    yield

            def qkv(b):
                for i in range(STEPS["qkv"]):
                    if 2 <= i < 2 + KQ:
                        m = i - 2
                        act.wait_ge(qkv_mm.sem, qkv_mm.at(b, m + 1))
                        act.activation(qT[:, m, :], ps[:, BANK_P + m % 2, 0:NB], ACT.Copy, scale=float(HD) ** -0.5).then_inc(q_ready.sem, 1)
                    yield

            def heads(b, ti):
                keys = P * (ti + 1)
                for i in range(STEPS["heads"]):
                    if i % 4 == 3 and i // 4 < H // 2:
                        j = i // 4
                        g = ti * H // 2 + j
                        act.wait_ge(max_ready.sem, max_ready.at(b, g + 1))
                        if g >= 1:
                            act.wait_ge(probsT_mm.sem, probsT_mm.at(b, g))
                        for e in range(2):
                            h = j // 4 * 8 + e * 4 + j % 4
                            act.activation(probs[:, e, 0:keys], ps[:, BANK_P + g % 2, e * T:e * T + keys], ACT.Exp, bias=nmax[:, e:e + 1],
                                           accum_out=psum_exp[:, ti, h:h + 1]).then_inc(probs_ready.sem, 1)
                    yield

            def idle(n):
                for i in range(n):
                    yield

            def up(b):
                for i in range(STEPS["up"]):
                    if 2 <= i < 2 + KF:
                        m = i - 2
                        act.wait_ge(up_mm.sem, up_mm.at(b, m + 1))
                        act.activation(hidden[:, m, :], ps[:, BANK_P + m % 2, 0:NB], ACT.Identity, bias=b1_col[:, m:m + 1]).then_inc(up_ready.sem, 1)
                    if i == 2 + KF:
                        act.wait_ge(up_ready.sem, up_ready.at(b, KF))
                        act.activation(hidden[:, :, :], hidden[:, :, :], ACT.Gelu).then_inc(gelu_ready.sem, 1)
                    yield

            def prepare(p, d):
                for i in range(STEPS["ins"]):
                    if 2 <= i < 2 + 2 * KI:
                        m = i - 2
                        dst = xsT[:, m, :] if m < KI else szT[:, d, m - KI, :]
                        act.wait_ge(in_mm.sem, in_mm.at(p, m + 1))
                        act.activation(dst, ps[:, BANK_P + m % 2, 0:NB], ACT.Copy).then_inc(in_raw.sem, 1)
                    if i == 2 + 2 * KI:
                        act.wait_ge(in_raw.sem, in_raw.at(p, 2 * KI))
                        act.activation(xsT[:, :, :], xsT[:, :, :], ACT.Silu).then_inc(in_ready.sem, 1)
                        act.activation(szT[:, d], szT[:, d], ACT.Silu).then_inc(in_ready.sem, 1)
                    yield
                for i in range(STEPS["dts"]):
                    if i % 2 == 1 and 5 <= i < 5 + 2 * KI:
                        m = (i - 5) // 2
                        act.wait_ge(dt_mm.sem, dt_mm.at(p, m + 1))
                        act.activation(pre[:, m, :], ps[:, BANK_P + (m + 1) % 2, 0:NB], ACT.Identity,
                                       bias=dtb_col[:, d, m:m + 1]).then_inc(pre_ready.sem, 1)
                    if i == 13:
                        act.wait_ge(abs_ready.sem, abs_ready.at(p, 1))
                        act.activation(expo, expo, ACT.Exp).then_inc(exp_ready.sem, 1)
                    if i == 15:
                        act.wait_ge(one_ready.sem, one_ready.at(p, 1))
                        act.activation(dt[:, d], u[:, d], ACT.Ln).then_inc(log_ready.sem, 1)
                    yield

            def glu(b):
                for i in range(STEPS["glu"]):
                    if 1 <= i < 1 + KG:
                        m = i - 1
                        act.wait_ge(glu_mm.sem, glu_mm.at(b, m + 1))
                        act.activation(gT[:, m, :], ps[:, BANK_P + m % 2, 0:NB], ACT.Copy).then_inc(glu_raw.sem, 1)
                    if i == 1 + KG:
                        act.wait_ge(glu_raw.sem, glu_raw.at(b, KG))
                        act.activation(gT[:, :, :], gT[:, :, :], ACT.Silu).then_inc(glu_silu.sem, 1)
                    yield

            def layer0(b):
                yield from norm(b, LN_ATT, hT)
                yield from qkv(b)
                yield from heads(b, 0)
                yield from heads(b, 1)
                yield from idle(STEPS["proj"])
                yield from norm(b, LN_MLP, hT)
                yield from up(b)
                yield from idle(STEPS["down"])
                yield from norm(b, LN_SSM, hT_ssm)

            def close(b):
                yield from norm(b, LN_GLU, hT)
                yield from glu(b)

            def take_B(r, i):
                act.wait_ge(BC_mm.sem, BC_mm.at(r, 1))
                act.wait_ge(uB_ready.sem, uB_ready.at(r, 2 - 2 * NR))
                act.activation(B_sb[:, i % NR, :], ps[:, BANK_BC + (i + 1) % 2, 0:NB], ACT.Copy).then_inc(B_ready.sem, 1)

            def scan_pass(b, d, last, chains, plan):
                p = 2 * b + d
                lo, hi = (1, NB) if d == 0 else (0, NB - 1)
                edge = 0 if d == 0 else NB - 1
                taken = set()

                def decays(i):
                    n, e = i // 2, i % 2
                    bank = ps[:, plan.bank[i], :]
                    if plan.before[i] is not None:
                        act.wait_ge(scan_done.sem, scan_done.at(p * NS + n, e + 1 - (i - plan.before[i])))
                    if i < 2 or plan.bank[i] >= BANK_P:
                        act.activation(bank.rearrange("p (k t) -> p k t", t=NB)[:, :, edge], zeros[:, :], ACT.Copy)
                    for c in range(2 * e, 2 * e + 2):
                        o = c % 2 * NB
                        done = act.activation(bank[:, o + lo:o + hi], dt[:, d, c, lo:hi], ACT.Exp, scale=A[:, d, c, n:n + 1])
                    done.then_inc(dA_ready.sem, 1)

                def state(n, e):
                    if n == 0 and e == 0:
                        act.wait_ge(u_ready.sem, u_ready.at(p, 1))
                    if e == 0 and n not in taken and not (last and n + AHEAD - 1 >= NS):
                        take_B(p * NS + n + AHEAD - 1, n + AHEAD - 1)
                    if plan.bank[2 * n + e] < BANK_P:
                        decays(2 * n + e)

                def before(j):
                    if j not in plan.ahead:
                        return
                    step = plan.steps[j][1]
                    if step == "norm":
                        s = LN_ATT if d == 0 else LN_MLP if j < plan.steps.index(("first", "up", 0)) else LN_SSM
                        act.wait_ge(norm_step[s].sem, norm_step[s].at(b + 1, 1))
                    elif step == "up":
                        act.wait_ge(up_ready.sem, up_ready.at(b + 1, KF))
                    elif step == "ins":
                        act.wait_ge(in_raw.sem, in_raw.at(p + 1, 2 * KI))
                    else:
                        act.wait_ge(glu_raw.sem, glu_raw.at(b - 1, KG))
                    for i in plan.ahead[j]:
                        decays(i)
                    n = (plan.ahead[j][0] - 1) // 2 + 1
                    if not (last and n + AHEAD - 1 >= NS):
                        taken.add(n)
                        take_B(p * NS + n + AHEAD - 1, n + AHEAD - 1)

                interleave(state, chains, plan, before)

            def period(b, has_prev, has_next):
                l0 = layer0(b + 1) if has_next else None

                def own():
                    yield from prepare(2 * b + 1, 1)

                def last(b, d):
                    yield from idle(STEPS["post"])
                    if d == 1:
                        yield from close(b)

                def backward():
                    yield from l0
                    yield from prepare(2 * b + 2, 0)

                forward = dict(first=l0, own=own(), last=last(b - 1, 1))
                plan = Plan(0, has_prev, has_next)
                scan_pass(b, 0, False, forward, plan)
                plan = Plan(1, has_prev, has_next)
                backwards = dict(first=backward(), last=last(b, 0))
                scan_pass(b, 1, not has_next, backwards, plan)

            for _ in layer0(0):
                pass
            for _ in prepare(0, 0):
                pass
            for i in range(AHEAD - 1):
                take_B(i, i)
            period(0, False, True)
            with act.Fori(1, NBLK - 1) as b:
                period(b, True, True)
            period(NBLK - 1, True, False)
            for _ in close(NBLK - 1):
                pass

        @block.vector
        def _(dve):
            setup = [0]

            def first(ins):
                setup[0] += 1
                ins.then_inc(dve_setup, 1)
                dve.wait_ge(dve_setup, setup[0])

            dve.memset(prime[:, 1:2], 0.0).then_inc(scan_done.sem, scan_done.start)
            dve.memset(prime[:, 2:3], 0.0).then_inc(hC_ready.sem, hC_ready.start)
            dve.memset(prime[:, 3:4], 0.0).then_inc(y_mm.sem, y_mm.start)
            dve.memset(prime[:, 4:5], 0.0).then_inc(uB_ready.sem, uB_ready.start)
            dve.memset(prime[:, 5:6], 0.0).then_inc(g_ready.sem, g_ready.start)
            dve.wait_ge(mods_mm, 1)
            dve.wait_ge(mods_in, N_MODS)
            dve.tensor_copy(mod_rows, ps[0:B, 1:3, :].rearrange("p a n -> p (a n)")).then_inc(rows_ready, 1)
            first(dve.tensor_tensor(mods[:, :, :, :].rearrange("p i k b -> p (i k) b"),
                                    ps[:, 0, 0:16 * B].rearrange("p (i b) -> p i b", b=B),
                                    mod_bias.rearrange("p i k -> p (i k)").unsqueeze(2).to_broadcast([P, 16, B]), ALU.add))
            for s in range(4):
                if s < 2:
                    gb = ln_g[:, s, :].unsqueeze(2).to_broadcast([P, KD, B])
                    bb = ln_b[:, s, :].unsqueeze(2).to_broadcast([P, KD, B])
                    first(dve.scalar_tensor_tensor(mod_scale[:, s], mods[:, 2 * s + 1], 1.0, gb, ALU.add, ALU.mult))
                    first(dve.scalar_tensor_tensor(mod_shift[:, s], mods[:, 2 * s + 1], 1.0, bb, ALU.add, ALU.mult))
                    first(dve.tensor_tensor(mod_shift[:, s], mod_shift[:, s], mods[:, 2 * s], ALU.add))
                else:
                    first(dve.tensor_scalar(mod_scale[:, s], mods[:, 2 * s + 1], 1.0, None, ALU.add))
                    first(dve.tensor_copy(mod_shift[:, s], mods[:, 2 * s]))
            dve.wait_ge(A_ready, 1)
            dve.tensor_scalar(A[:, :, :, :], A[:, :, :, :], -1.0, None, ALU.mult).then_inc(A_ready, 1)
            dve.wait_ge(consts_ready, 5)
            dve.wait_ge(weights_in, N_WEIGHTS)
            for d in range(2):
                for c in range(KI):
                    dve.tensor_scalar(skip_diag[:, d, c, :], ident[:, :], D_col[:, d, c:c + 1], None, ALU.mult).then_inc(mods_ready, 1)
            dve.wait_ge(x_in, 16)

            def x_tile(b, j):
                return xs_all[:, bass.ds(b * TT + j, 1), :].rearrange("p a d -> p (a d)")

            def norm(b, s, before):
                for i in range(STEPS["norm"]):
                    if i == 0:
                        dve.wait_ge(x_in, 16)
                        if before is not None:
                            dve.wait_ge(before[0].sem, before[0].at(before[1], 1))
                        for j in range(TT):
                            last = dve.bn_stats(stats[:, j, :], x_tile(b, j))
                        last.then_inc(norm_step[s].sem, 1)
                        dve.wait_ge(norm_step[s].sem, norm_step[s].at(b, 1))
                        dve.sem_inc(bn_turns)
                        for j in range(TT):
                            last = dve.bn_aggr(mv[:, j, :], stats[:, j, :])
                        last.then_inc(norm_step[s].sem, 1)
                        dve.wait_ge(norm_step[s].sem, norm_step[s].at(b, 2))
                        dve.tensor_scalar(mv[:, :, 1], mv[:, :, 1], EPS, None, ALU.add).then_inc(stat_ready[s].sem, 1)
                    if i == 3:
                        dve.wait_ge(std_ready[s].sem, std_ready[s].at(b, 1))
                        dve.reciprocal(rstd[:, :], rstd[:, :]).then_inc(norm_step[s].sem, 1)
                        dve.wait_ge(norm_step[s].sem, norm_step[s].at(b, 3))
                        for j in range(TT):
                            last = dve.tensor_scalar(xn[:, j, :], x_tile(b, j), mv[:, j, 0:1], rstd[:, j:j + 1], ALU.subtract, ALU.mult)
                        last.then_inc(xn_ready[s].sem, 1)
                    yield

            def residual(b, bank, rnd, gates, which, gate_in, mm, mul, done):
                dve.wait_ge(gate_in.sem, gate_in.at(b, 16))
                dve.wait_ge(mm.sem, mm.at(rnd, 1))
                dve.tensor_tensor(part[:, :, :], ps[:, bank, :].rearrange("p (j d) -> p j d", d=D),
                                  gates[:, which:which + 1, :].to_broadcast([P, TT, D]), ALU.mult).then_inc(mul.sem, 1)
                dve.wait_ge(mul.sem, mul.at(rnd, 1))
                xt = xs_all[:, bass.ds(b * TT, TT), :]
                dve.tensor_tensor(xt, xt, part[:, :, :], ALU.add).then_inc(done.sem, 1)

            def qkv(b):
                for i in range(STEPS["qkv"]):
                    m = i - 1
                    if KQ <= m < 2 * KQ:
                        dve.wait_ge(qkv_mm.sem, qkv_mm.at(b, m + 1))
                        dve.tensor_copy(kT[:, m - KQ, :], ps[:, BANK_P + m % 2, 0:NB]).then_inc(kv_ready.sem, 1)
                    if 2 * KQ <= m < 2 * KQ + TT:
                        dve.wait_ge(qkv_mm.sem, qkv_mm.at(b, m + 1))
                        dve.tensor_copy(v[:, m - 2 * KQ, :], ps[:, BANK_P + m % 2, 0:D]).then_inc(kv_ready.sem, 1)
                    yield

            def heads(b, ti):
                keys, nk = P * (ti + 1), ti + 1
                for i in range(STEPS["heads"]):
                    if i % 4 == 3 and 1 <= i // 4 < 1 + H // 2:
                        j = i // 4 - 1
                        g = ti * H // 2 + j
                        h = j // 4 * 8 + j % 4
                        dve.wait_ge(pv_mm.sem, pv_mm.at(b, g + 1))
                        dve.tensor_copy(o_sb[:, ti, :].rearrange("p (a c e) -> p a c e", c=4, e=HD)[:, 2 * (j // 4):2 * (j // 4) + 2, j % 4, :],
                                        ps[:, BANK_P + g % 2, 0:2 * HD].rearrange("p (a e) -> p a e", e=HD)).then_inc(o_raw.sem, 1)
                    if i % 4 == 1 and 1 <= i // 4 < 1 + H // 2:
                        g = ti * H // 2 + i // 4 - 1
                        dve.wait_ge(probsT_mm.sem, probsT_mm.at(b, g + 1))
                        if g >= 1:
                            dve.wait_ge(pv_mm.sem, pv_mm.at(b, g))
                        dve.tensor_copy(probsT[:, 0:nk * 2 * P], ps[:, BANK_P + g % 2, 0:nk * 2 * P]).then_inc(probsT_ready.sem, 1)
                    if i % 4 == 1 and i // 4 < H // 2:
                        g = ti * H // 2 + i // 4
                        dve.wait_ge(score_mm.sem, score_mm.at(b, g + 1))
                        if g >= 1:
                            dve.wait_ge(probs_ready.sem, probs_ready.at(b, 2 * g))
                        dve.tensor_reduce(nmax[:, :], ps[:, BANK_P + g % 2, :].rearrange("p (e t) -> p e t", t=T)[:, :, 0:keys],
                                          AX.X, ALU.max, negate=True).then_inc(max_ready.sem, 1)
                    if i == STEPS["heads"] - 1:
                        dve.wait_ge(probs_ready.sem, probs_ready.at(b, (ti + 1) * H))
                        dve.reciprocal(rsum[:, ti, :], psum_exp[:, ti, :]).then_inc(rsum_ready.sem, 1)
                        dve.wait_ge(rsum_ready.sem, rsum_ready.at(b, ti + 1))
                        dve.wait_ge(o_raw.sem, o_raw.at(b, (ti + 1) * H // 2))
                        o = o_sb[:, ti, :].rearrange("p (h e) -> p h e", e=HD)
                        dve.tensor_tensor(o, o, rsum[:, ti, :].unsqueeze(2).to_broadcast([P, H, HD]), ALU.mult).then_inc(o_ready.sem, 1)
                    yield

            def project(b):
                for i in range(STEPS["proj"]):
                    if i == 1:
                        dve.wait_ge(oT_mm.sem, oT_mm.at(b, 1))
                        dve.tensor_copy(oT[:, :, :].rearrange("p a n -> p (a n)"), ps[:, BANK_P, :]).then_inc(oT_ready.sem, 1)
                    if i == 4:
                        residual(b, BANK_P + 1, b, gate_l0, 0, gate0_in, res_mm[RES_ATT], res_part[RES_ATT], res_done[RES_ATT])
                    yield

            def idle(n):
                for i in range(n):
                    yield

            def down(b):
                for i in range(STEPS["down"]):
                    if i == STEPS["down"] - 1:
                        residual(b, BANK_P, b, gate_l0, 1, gate0_in, res_mm[RES_MLP], res_part[RES_MLP], res_done[RES_MLP])
                    yield

            def prepare(p, d):
                yield from idle(STEPS["ins"])
                for i in range(STEPS["dts"]):
                    bc = ps[:, BANK_P, 0:NB]
                    if i == 2:
                        dve.wait_ge(bc_mm.sem, bc_mm.at(p, 1))
                        dve.tensor_copy(bc_parts[:, 0, :], bc).then_inc(bc_step.sem, 1)
                        dve.wait_ge(bc_step.sem, bc_step.at(p, 1))
                        dve.tensor_tensor(bc_rest, bc, bc_parts[:, 0, :], ALU.subtract).then_inc(bc_step.sem, 1)
                    if i == 3:
                        dve.wait_ge(bc_step.sem, bc_step.at(p, 2))
                        dve.tensor_copy(bc_parts[:, 1, :], bc_rest).then_inc(bc_step.sem, 1)
                        dve.wait_ge(bc_step.sem, bc_step.at(p, 3))
                        dve.tensor_tensor(bc_rest, bc_rest, bc_parts[:, 1, :], ALU.subtract).then_inc(bc_step.sem, 1)
                        dve.wait_ge(bc_step.sem, bc_step.at(p, 4))
                        dve.tensor_copy(bc_parts[:, 2, :], bc_rest).then_inc(bc_ready.sem, 1)
                    if i == 12:
                        dve.wait_ge(pre_ready.sem, pre_ready.at(p, KI))
                        dve.scalar_tensor_tensor(expo, pre, -1.0, pre, ALU.mult, ALU.min).then_inc(abs_ready.sem, 1)
                    if i == 14:
                        dve.wait_ge(exp_ready.sem, exp_ready.at(p, 1))
                        dve.tensor_scalar(u[:, d], expo, 1.0, None, ALU.add).then_inc(one_ready.sem, 1)
                    if i == 15:
                        dve.wait_ge(one_ready.sem, one_ready.at(p, 1))
                        dve.scalar_tensor_tensor(expo, u[:, d], -1.0, expo, ALU.add, ALU.subtract).then_inc(soft_step.sem, 1)
                    if i == 16:
                        dve.wait_ge(soft_step.sem, soft_step.at(p, 1))
                        dve.scalar_tensor_tensor(pre, pre, 0.0, expo, ALU.max, ALU.subtract).then_inc(soft_step.sem, 1)
                    if i == 17:
                        dve.wait_ge(soft_step.sem, soft_step.at(p, 2))
                        dve.wait_ge(log_ready.sem, log_ready.at(p, 1))
                        dve.tensor_tensor(dt[:, d], dt[:, d], pre, ALU.add).then_inc(dt_ready.sem, 1)
                    if i == 18:
                        dve.wait_ge(dt_ready.sem, dt_ready.at(p, 1))
                        dve.wait_ge(in_ready.sem, in_ready.at(p, 1))
                        dve.tensor_tensor(u[:, d], dt[:, d], xsT[:, :, :], ALU.mult).then_inc(u_ready.sem, 1)
                    yield

            def post(b, d):
                for i in range(STEPS["post"]):
                    if i == 5:
                        residual(b, BANK_P, 2 * b + d, gate_l1, GATE_SSM, gate1_in, post_mm, post_part, post_done)
                    yield

            def glu(b):
                for i in range(STEPS["glu"]):
                    if 7 <= i < 7 + KG:
                        m = i - 7
                        dve.wait_ge(glu_silu.sem, glu_silu.at(b, 1))
                        dve.wait_ge(glu_mm.sem, glu_mm.at(b, KG + m + 1))
                        dve.tensor_tensor(gT[:, m, :], ps[:, BANK_P + m % 2, 0:NB], gT[:, m, :], ALU.mult).then_inc(glu_ready.sem, 1)
                    if i == STEPS["glu"] - 1:
                        residual(b, BANK_P, b, gate_l1, GATE_GLU, gate1_in, res_mm[RES_GLU], res_part[RES_GLU], res_done[RES_GLU])
                    yield

            def layer0(b):
                yield from norm(b, LN_ATT, None)
                yield from qkv(b)
                yield from heads(b, 0)
                yield from heads(b, 1)
                yield from project(b)
                yield from norm(b, LN_MLP, (res_done[RES_ATT], b))
                yield from idle(STEPS["up"])
                yield from down(b)
                yield from norm(b, LN_SSM, (res_done[RES_MLP], b))

            def close(b):
                yield from norm(b, LN_GLU, (post_done, 2 * b + 1))
                yield from glu(b)

            def times_C(r, i, e, last):
                if e == 0 and last:
                    dve.wait_ge(BC_mm.sem, BC_mm.at(r + AHEAD, 1))
                elif e == 0:
                    dve.wait_ge(B_ready.sem, B_ready.at(r + AHEAD, 1))
                dve.wait_ge(scan_done.sem, scan_done.at(r, e + 1))
                h = hst[:, i % NR, 2 * e:2 * e + 2, :]
                C = ps[:, BANK_BC + i % 2:BANK_BC + i % 2 + 1, NB:2 * NB].to_broadcast([P, 2, NB])
                dve.tensor_tensor(h, h, C, ALU.mult).then_inc(hC_ready.sem, 1)

            def gate_y(p, d):
                dve.wait_ge(y_mm.sem, y_mm.at(p * NS + (NS - 1), 1))
                dve.wait_ge(in_ready.sem, in_ready.at(p, 2))
                dve.tensor_tensor(gT[:, :, :].rearrange("p k n -> p (k n)"), ps[:, BANK_Y:BANK_Y + 2, :].rearrange("p a n -> p (a n)"),
                                  szT[:, d].rearrange("p k n -> p (k n)"), ALU.mult).then_inc(g_ready.sem, 1)

            def state_of(p, d, very_first, very_last, plan):
                way = slice(None) if d == 0 else slice(None, None, -1)

                def state(n, e):
                    r = p * NS + n
                    if n == BEHIND and e == 0 and not very_first:
                        gate_y(p - 1, 1 - d)
                    dve.wait_ge(uB_ready.sem, uB_ready.at(r, e + 1))
                    if e == 0:
                        dve.wait_ge(y_mm.sem, y_mm.at(r, 1 - NR))
                    dve.wait_ge(dA_ready.sem, dA_ready.at(r, e + 1))
                    pair = lambda t: t[:, 2 * e:2 * e + 2, :].rearrange("p k n -> p (k n)")[:, way]
                    dve.tensor_tensor_scan(pair(hst[:, n % NR]), ps[:, plan.bank[2 * n + e], :][:, way],
                                           uB[:, (2 * n + e) % NU].rearrange("p k n -> p (k n)")[:, way],
                                           0.0, ALU.mult, ALU.add).then_inc(scan_done.sem, 1)
                    if not (very_first and n == 0):
                        times_C(r - 1, n + NR - 1, e, very_last and n - 1 + AHEAD >= NS)

                return state

            def period(b, has_prev, has_next):
                l0 = layer0(b + 1) if has_next else None

                def own():
                    yield from prepare(2 * b + 1, 1)

                def last(b, d):
                    yield from post(b, d)
                    if d == 1:
                        yield from close(b)

                def backward():
                    yield from l0
                    yield from prepare(2 * b + 2, 0)

                forward = dict(first=l0, own=own(), last=last(b - 1, 1))
                plan = Plan(0, has_prev, has_next)
                interleave(state_of(2 * b, 0, not has_prev, False, plan), forward, plan)
                plan = Plan(1, has_prev, has_next)
                backwards = dict(first=backward(), last=last(b, 0))
                interleave(state_of(2 * b + 1, 1, False, not has_next, plan), backwards, plan)

            for _ in layer0(0):
                pass
            for _ in prepare(0, 0):
                pass
            period(0, False, True)
            with dve.Fori(1, NBLK - 1) as b:
                period(b, True, True)
            period(NBLK - 1, True, False)
            for e in range(2):
                times_C(2 * NBLK * NS - 1, NS - 1, e, True)
            gate_y(2 * NBLK - 1, 1)
            for _ in post(NBLK - 1, 1):
                pass
            for _ in close(NBLK - 1):
                pass

        @block.tensor
        def _(pe):
            pe.wait_ge(silu_ready, 1)
            pe.wait_ge(mods_in, N_MODS)
            pe.wait_ge(consts_ready, 5)
            of_kind = [(wada, 1, 0), (wada, 1, 1), (wada, 1, 3), (wada, 1, 4),
                       (wada1[0], 0, 0), (wada1[0], 0, 1), (wada1[1], 0, 0), (wada1[1], 0, 1)]
            conds = (cond_col, silu_col)
            for i, (w, cn, col) in enumerate(of_kind):
                for m in range(KD):
                    o = (i * KD + m) * B
                    for k in range(KD):
                        pe.matmul(ps[:, 0, o:o + B], w[:, k, col * D + m * P:col * D + (m + 1) * P], conds[cn][:, k, :],
                                  start=(k == 0), stop=(k == KD - 1))
            for i, (w, cn, col) in enumerate(((wada, 1, 2), (wada, 1, 5), (wada1[0], 0, 2), (wada1[1], 0, 2))):
                o = ps[0:B, 1 + i // 2, (i % 2) * D:(i % 2 + 1) * D]
                for k in range(KD):
                    pe.matmul(o, conds[cn][:, k, :], w[:, k, col * D:(col + 1) * D], start=(k == 0), stop=False)
                last = pe.matmul(o, ones_row[:, 0:B], gate_bias[:, i, :], start=False, stop=True)
            last.then_inc(mods_mm, 1)
            pe.wait_ge(rows_ready, 1)
            pe.wait_ge(weights_in, N_WEIGHTS)
            pe.wait_ge(mods_ready, 2 * KI)

            def idle(n):
                for i in range(n):
                    yield

            def transpose_block(src):
                for c in range(KD):
                    for j in range(TT):
                        last = pe.transpose(ps[:, BANK_P, c * NB + j * P:c * NB + (j + 1) * P], src[:, j, c * P:(c + 1) * P], ident[:, :])
                return last

            def product(i, lhsT, rhs, ks, kn):
                for k in ks:
                    last = pe.matmul(ps[:, BANK_P + i % 2, 0:NB], lhsT(k), rhs[:, k, :], start=(k == 0), stop=(k == kn - 1))
                return last

            def to_tokens(bank, j, act_T, w, ks, kn, bias=None):
                o = ps[:, bank, j * D:(j + 1) * D]
                if bias is not None and ks[0] == 0:
                    pe.matmul(o, ones_row[:, :], bias, start=True, stop=False)
                for k in ks:
                    last = pe.matmul(o, act_T[:, k, j * P:(j + 1) * P], w[:, k, :], start=(k == 0 and bias is None), stop=(k == kn - 1))
                return last

            def norm(b, s):
                for i in range(STEPS["norm"]):
                    if i == 4:
                        pe.wait_ge(xn_ready[s].sem, xn_ready[s].at(b, 1))
                        transpose_block(xn).then_inc(xnT_mm[s].sem, 1)
                    yield

            def qkv(b):
                for i in range(STEPS["qkv"]):
                    if i == 0:
                        pe.wait_ge(hT_ready[LN_ATT].sem, hT_ready[LN_ATT].at(b, 1))
                    if 2 <= i < 2 + KQ:
                        pe.wait_ge(q_ready.sem, q_ready.at(b, i - 1))
                    elif 2 + KQ <= i < 10:
                        pe.wait_ge(kv_ready.sem, kv_ready.at(b, i - 1 - KQ))
                    if i < 2 * KQ:
                        w, m = (wq, i) if i < KQ else (wk, i - KQ)
                        product(i, lambda k: w[:, k, 4 * m:4 * m + 4, :].rearrange("p h e -> p (h e)"), hT, range(KD), KD).then_inc(qkv_mm.sem, 1)
                    elif i < 2 * KQ + TT:
                        j = i - 2 * KQ
                        for k in range(KD):
                            last = pe.matmul(ps[:, BANK_P + i % 2, 0:D], hT[:, k, j * P:(j + 1) * P], wv[:, k, :], start=(k == 0), stop=(k == KD - 1))
                        last.then_inc(qkv_mm.sem, 1)
                    yield

            def heads(b, ti):
                keys, nk = P * (ti + 1), ti + 1
                for i in range(STEPS["heads"]):
                    if i % 4 == 2 and 1 <= i // 4 < 1 + H // 2:
                        j = i // 4 - 1
                        g = ti * H // 2 + j
                        pe.wait_ge(probsT_ready.sem, probsT_ready.at(b, g + 1))
                        for e in range(2):
                            h = j // 4 * 8 + e * 4 + j % 4
                            for k in range(nk):
                                last = pe.matmul(ps[:, BANK_P + g % 2, e * HD:(e + 1) * HD], probsT[:, (k * 2 + e) * P:(k * 2 + e + 1) * P],
                                                 v[:, k, h * HD:(h + 1) * HD], start=(k == 0), stop=(k == nk - 1))
                        last.then_inc(pv_mm.sem, 1)
                    if i % 4 == 0 and 1 <= i // 4 < 1 + H // 2:
                        g = ti * H // 2 + i // 4 - 1
                        pe.wait_ge(probs_ready.sem, probs_ready.at(b, 2 * (g + 1)))
                        for k in range(nk):
                            for e in range(2):
                                o = (k * 2 + e) * P
                                last = pe.transpose(ps[:, BANK_P + g % 2, o:o + P], probs[:, e, k * P:(k + 1) * P], ident[:, :])
                        last.then_inc(probsT_mm.sem, 1)
                    if i % 4 == 0 and i // 4 < H // 2:
                        j = i // 4
                        g = ti * H // 2 + j
                        if g == 0:
                            pe.wait_ge(q_ready.sem, q_ready.at(b, KQ))
                            pe.wait_ge(kv_ready.sem, kv_ready.at(b, KQ + TT))
                        if g >= 2:
                            pe.wait_ge(o_raw.sem, o_raw.at(b, g - 1))
                        rows = slice(HP * (j % 4), HP * (j % 4 + 1))
                        for e in range(2):
                            c = j // 4 * 2 + e
                            pe.matmul(ps[:, BANK_P + g % 2, e * T:e * T + keys], qT[rows, c, ti * P:(ti + 1) * P], kT[rows, c, 0:keys],
                                      start=True, stop=False)
                            last = pe.matmul(ps[:, BANK_P + g % 2, e * T + ti * P:e * T + (ti + 1) * P], ident_b[:, :], causal_b[:, :],
                                             start=False, stop=True)
                        last.then_inc(score_mm.sem, 1)
                    yield

            def project(b):
                for i in range(STEPS["proj"]):
                    if i == 0:
                        pe.wait_ge(o_ready.sem, o_ready.at(b, TT))
                        transpose_block(o_sb).then_inc(oT_mm.sem, 1)
                    if i in (1, 2):
                        pe.wait_ge(oT_ready.sem, oT_ready.at(b, 1))
                        last = to_tokens(BANK_P + 1, i - 1, oT, wproj, range(KD), KD, bias_rows[:, 0, :])
                        if i == 2:
                            last.then_inc(res_mm[RES_ATT].sem, 1)
                    yield

            def up(b):
                for i in range(STEPS["up"]):
                    if i == 0:
                        pe.wait_ge(hT_ready[LN_MLP].sem, hT_ready[LN_MLP].at(b, 1))
                    if i < KF:
                        if i >= 2:
                            pe.wait_ge(up_ready.sem, up_ready.at(b, i - 1))
                        product(i, lambda k: w1[:, k, i * P:(i + 1) * P], hT, range(KD), KD).then_inc(up_mm.sem, 1)
                    yield

            def down(b):
                for i in range(STEPS["down"]):
                    if i == 0:
                        pe.wait_ge(gelu_ready.sem, gelu_ready.at(b, 1))
                    if i < 8:
                        last = to_tokens(BANK_P, i // 4, hidden, w2, range(i % 4 * 2, i % 4 * 2 + 2), KF, bias_rows[:, 1, :])
                        if i == 7:
                            last.then_inc(res_mm[RES_MLP].sem, 1)
                    yield

            def prepare(p, d, b):
                for i in range(STEPS["ins"]):
                    if i == 0:
                        pe.wait_ge(hT_ready[LN_SSM].sem, hT_ready[LN_SSM].at(b, 1))
                    if i < 2 * KI:
                        if i >= 2:
                            pe.wait_ge(in_raw.sem, in_raw.at(p, i - 1))
                        product(i, lambda k: w_in[d][:, k, i * P:(i + 1) * P], hT_ssm, range(KD), KD).then_inc(in_mm.sem, 1)
                    yield
                for i in range(STEPS["dts"]):
                    if i == 0:
                        pe.wait_ge(in_ready.sem, in_ready.at(p, 1))
                    if i < 2 + 2 * KI:
                        m = i // 2 - 1 if i >= 2 else KI
                        bank = i // 2 % 2
                        if i in (4, 5):
                            pe.wait_ge(bc_step.sem, bc_step.at(p, 2))
                        if i >= 6 and i % 2 == 0:
                            pe.wait_ge(pre_ready.sem, pre_ready.at(p, m - 1))
                        last = product(bank, lambda k: w_xp[d][:, k, m * P:(m + 1) * P], xsT, range(i % 2 * 2, i % 2 * 2 + 2), KI)
                        if i == 1:
                            last.then_inc(bc_mm.sem, 1)
                        elif i % 2 == 1:
                            last.then_inc(dt_mm.sem, 1)
                    yield

            def post(b, d):
                for i in range(STEPS["post"]):
                    if i == 0:
                        pe.wait_ge(g_ready.sem, g_ready.at(2 * b + d, 1))
                    if i < 4:
                        last = to_tokens(BANK_P, i // 2, gT, w_out[d], range(i % 2 * 2, i % 2 * 2 + 2), KI)
                        if i == 3:
                            last.then_inc(post_mm.sem, 1)
                    if i == 6:
                        pe.wait_ge(post_part.sem, post_part.at(2 * b + d, 1))
                    yield

            def glu(b):
                for i in range(STEPS["glu"]):
                    if i == 0:
                        pe.wait_ge(hT_ready[LN_GLU].sem, hT_ready[LN_GLU].at(b, 1))
                    if i < KG:
                        if i >= 2:
                            pe.wait_ge(glu_raw.sem, glu_raw.at(b, i - 1))
                        product(i, lambda k: wg1[:, k, i * P:(i + 1) * P], hT, range(KD), KD).then_inc(glu_mm.sem, 1)
                    if 6 <= i < 6 + KG:
                        m = i - 6
                        if m < 2:
                            pe.wait_ge(glu_raw.sem, glu_raw.at(b, KG - 1 + m))
                        else:
                            pe.wait_ge(glu_ready.sem, glu_ready.at(b, m - 1))
                        product(m, lambda k: wg2[:, k, m * P:(m + 1) * P], hT, range(KD), KD).then_inc(glu_mm.sem, 1)
                    if 11 <= i < 15:
                        if i == 11:
                            pe.wait_ge(glu_ready.sem, glu_ready.at(b, KG))
                        last = to_tokens(BANK_P, (i - 11) // 2, gT, wg3, range((i - 11) % 2 * 2, (i - 11) % 2 * 2 + 2), KG)
                        if i == 14:
                            last.then_inc(res_mm[RES_GLU].sem, 1)
                    yield

            def layer0(b):
                yield from norm(b, LN_ATT)
                yield from qkv(b)
                yield from heads(b, 0)
                yield from heads(b, 1)
                yield from project(b)
                yield from norm(b, LN_MLP)
                yield from up(b)
                yield from down(b)
                yield from norm(b, LN_SSM)

            def close(b):
                yield from norm(b, LN_GLU)
                yield from glu(b)

            def spread(bank, side, d, group, n):
                return pe.matmul(ps[:, bank, side * NB:(side + 1) * NB], pick[0:PARTS * HP, n % HP:n % HP + 1].to_broadcast([PARTS * HP, P]),
                                 bc_rows[:, d, group + n // HP, :], start=True, stop=True)

            def spread_B(p, d, n):
                r = p * NS + n
                if n == 0:
                    pe.wait_ge(bc_in.sem, bc_in.at(p, bc_in.per))
                pe.wait_ge(B_ready.sem, B_ready.at(r, -1))
                return spread(BANK_BC + (n + 1) % 2, 0, d, 0, n)

            def spread_BC(p, d, n, last):
                pe.wait_ge(hC_ready.sem, hC_ready.at(p * NS + n, 2 - 2 * 2))
                if n + AHEAD < NS:
                    spread_B(p, d, n + AHEAD)
                elif not last:
                    spread_B(p + 1, 1 - d, n + AHEAD - NS)
                spread(BANK_BC + n % 2, 1, d, 2, n).then_inc(BC_mm.sem, 1)

            def start_y(p, d):
                pe.wait_ge(g_ready.sem, g_ready.at(p, 0))
                for c in range(KI):
                    pe.matmul(ps[:, BANK_Y + c // 2, c % 2 * NB:(c % 2 + 1) * NB], skip_diag[:, d, c, :], xsT[:, c, :],
                              start=(c % 2 == 0), stop=False, skip_group_check=True)

            def sum_state(r, n, e):
                pe.wait_ge(hC_ready.sem, hC_ready.at(r, e + 1))
                last = pe.matmul(ps[:, BANK_Y + e, :], ident[:, :], hst[:, n % NR, 2 * e:2 * e + 2, :].rearrange("p k n -> p (k n)"),
                                 start=False, stop=(n == NS - 1), skip_group_check=True)
                if e == 1:
                    last.then_inc(y_mm.sem, 1)

            def state_of(p, d, very_first, very_last):
                def state(n, e):
                    if e == 0:
                        spread_BC(p, d, n, very_last)
                        if n == BEHIND:
                            start_y(p, d)
                    if n >= BEHIND:
                        sum_state(p * NS + n - BEHIND, n - BEHIND, e)
                    elif not very_first:
                        sum_state(p * NS + n - BEHIND, NS + n - BEHIND, e)

                return state

            def period(b, has_prev, has_next):
                l0 = layer0(b + 1) if has_next else None

                def own():
                    yield from prepare(2 * b + 1, 1, b)

                def last(b, d):
                    yield from post(b, d)
                    if d == 1:
                        yield from close(b)

                def backward():
                    yield from l0
                    yield from prepare(2 * b + 2, 0, b + 1)

                def free(d, plan):
                    p = 2 * b + d

                    def before(j):
                        if j in plan.scanned:
                            n, e = plan.scanned[j] // 2, plan.scanned[j] % 2
                            pe.wait_ge(scan_done.sem, scan_done.at(p * NS + n, e + 1))
                        if plan.steps[j] == ("last", "post", 0) and d == 0:
                            pe.wait_ge(in_raw.sem, in_raw.at(p + 1, 2 * KI))
                        if plan.steps[j] == ("last", "post", 0) and d == 1 and has_next:
                            pe.wait_ge(pre_ready.sem, pre_ready.at(p + 1, KI))
                        if plan.steps[j] == ("last", "norm", 4):
                            pe.wait_ge(pre_ready.sem, pre_ready.at(p + 1, KI))

                    return before

                forward = dict(first=l0, own=own(), last=last(b - 1, 1))
                plan = Plan(0, has_prev, has_next)
                interleave(state_of(2 * b, 0, not has_prev, False), forward, plan, free(0, plan))
                plan = Plan(1, has_prev, has_next)
                backwards = dict(first=backward(), last=last(b, 0))
                interleave(state_of(2 * b + 1, 1, False, not has_next), backwards, plan, free(1, plan))

            for _ in layer0(0):
                pass
            for _ in prepare(0, 0, 0):
                pass
            for n in range(AHEAD):
                spread_B(0, 0, n).then_inc(BC_mm.sem, 1)
            period(0, False, True)
            with pe.Fori(1, NBLK - 1) as b:
                period(b, True, True)
            period(NBLK - 1, True, False)
            for n in range(NS - BEHIND, NS):
                for e in range(2):
                    sum_state((2 * NBLK - 1) * NS + n, n, e)
            for _ in post(NBLK - 1, 1):
                pass
            for _ in close(NBLK - 1):
                pass


_MATRICES = ['L0_cond_Wqkv', 'L0_cond_Wproj', 'L0_cond_W1', 'L0_cond_W2', 'L0_cond_Wada', 'L1_cond_adaln_mamba_w',
             'L1_cond_adaln_mlp_w', 'L1_cond_mlp_w1', 'L1_cond_mlp_w2', 'L1_cond_mlp_w3',
             'L1_cond_fwd_in_w', 'L1_cond_fwd_xproj_w', 'L1_cond_fwd_out_w',
             'L1_cond_bwd_in_w', 'L1_cond_bwd_xproj_w', 'L1_cond_bwd_out_w']


def kernel(**inputs):
    import numpy as _np
    import concourse.bacc as _bacc
    from concourse import mybir as _mybir
    from concourse.bass_utils import run_bass_kernel_spmd as _run

    get = lambda name: _np.asarray(inputs[name])
    P, D = 128, 256
    third = lambda name, i: get(name)[i * D:(i + 1) * D]
    by_channel = lambda a: a.reshape(-1, P).T
    l0, l1, mamba, glu = 'L0_cond_', 'L1_cond_', 'L1_cond_adaln_mamba_b', 'L1_cond_adaln_mlp_b'
    shifts = [third(l0 + 'bada', i) for i in (0, 1, 3, 4)] + [third(mamba, 0), third(mamba, 1), third(glu, 0), third(glu, 1)]
    cond = get('cond_1024')
    columns = _np.concatenate(
        [cond[:, k * P:(k + 1) * P].T for k in range(D // P)] + [by_channel(a) for a in shifts + [
            get(l0 + 'g1'), get(l0 + 'g2'), get(l0 + 'be1'), get(l0 + 'be2'), get(l0 + 'b1'),
            get(l1 + 'fwd_dt_bias'), get(l1 + 'bwd_dt_bias'), get(l1 + 'fwd_D'), get(l1 + 'bwd_D')]], axis=1)
    rows = _np.concatenate([third(l0 + 'bada', 2), third(l0 + 'bada', 5), third(mamba, 2), third(glu, 2),
                            get(l0 + 'bproj'), get(l0 + 'b2')])[None, :]
    A_log = _np.concatenate([get(l1 + n + 'A_log')[k * P:(k + 1) * P] for n in ('fwd_', 'bwd_') for k in range(4)], axis=1)

    nc = _bacc.Bacc("TRN2", target_bir_lowering=False, num_devices=1)
    arrays, args = {}, []
    for name, a in [('x', get('x')), ('columns', columns), ('rows', rows), ('A_log', A_log)] + [(n, get(n)) for n in _MATRICES]:
        a = _np.ascontiguousarray(a)
        arrays[f"in_{name}_dram"] = a
        args.append(nc.dram_tensor(f"in_{name}_dram", a.shape, _mybir.dt.from_np(a.dtype), kind="ExternalInput").ap())
    args.append(nc.dram_tensor("out_0_dram", get('x').shape, _mybir.dt.float32, kind="ExternalOutput").ap())
    args.append(nc.dram_tensor("gate_rows_dram", (cond.shape[0], 4 * D), _mybir.dt.float32, kind="Internal").ap())
    cond_transformer_mamba_kernel(nc, *args)
    r = _run(nc, [arrays], core_ids=[0])
    return r.results[0]["out_0_dram"]
```
